# Optimizing a Trainium2 kernel written in Bass

```python
import numpy as np
import jax
import jax.numpy as jnp

def _softmax(x, axis=-1):
    return jax.nn.softmax(x, axis=axis)
def _gelu(x):
    return jax.nn.gelu(x, approximate=True)
def _silu(x):
    return jax.nn.silu(x)
def _sigmoid(x):
    return jax.nn.sigmoid(x)
def _layernorm(x, axis=-1, eps=1e-5):
    m = jnp.mean(x, axis=axis, keepdims=True)
    v = jnp.var(x, axis=axis, keepdims=True)
    return (x - m) / jnp.sqrt(v + eps)
def _scatter_add(tgt, idx, src, axis=0):
    return tgt.at[idx].add(src)
def _segment_sum(src, seg, n):
    return jax.ops.segment_sum(src, seg, n)

kernel_name = 'mk_conv_seq_d1_conv_nchw128_aab832'

def setup_inputs(seed: int = 0):
    np.random.seed(seed)
    _w = jnp.asarray
    def _rec_inputs():
        import jax
        import jax.numpy as jnp
        _gk = jax.random.key(seed)
        x = -0.0002928 + 1 * jax.random.normal(jax.random.fold_in(_gk, 1), (8, 128, 64, 64), jnp.float32)
        return x
    x = _rec_inputs()
    def _L0_conv_setup():
        import math
        import jax, jax.numpy as jnp
        import numpy as np

        def _unfold(x, kh, kw, dh, dw, ph, pw):
            n, c, h, w = x.shape
            xp = jnp.pad(x, ((0, 0), (0, 0), (ph, ph), (pw, pw)))
            patches = jnp.stack([xp[:, :, i * dh:i * dh + h, j * dw:j * dw + w] for i in range(kh) for j in range(kw)], axis=2)
            return patches
        key = jax.random.key(seed)
        k1, k2, k3, k4 = jax.random.split(key, 4)
        n, c, h, w = (8, 128, 64, 64)
        x = jax.random.normal(k1, (n, c, h, w), dtype=jnp.float32)
        p1_w = 0.1 * jax.random.normal(k2, (1, c, h, 1), dtype=jnp.float32)
        p7_w = jax.random.normal(k3, (c, c), dtype=jnp.float32) / np.sqrt(c)
        p10_w = jax.random.normal(k4, (c * 21, c // 4), dtype=jnp.float32) / np.sqrt(c // 4)
        return {'x': x, 'p1_w': p1_w, 'p7_w': p7_w, 'p10_w': p10_w}
    _L0_conv_all = _L0_conv_setup()
    _L0_conv_in = {k: v for k, v in _L0_conv_all.items() if k in ('p1_w', 'p7_w', 'p10_w', )}
    del _L0_conv_all

    return {
        "x": x,
        "L0_conv_p1_w": _L0_conv_in["p1_w"],
        "L0_conv_p7_w": _L0_conv_in["p7_w"],
        "L0_conv_p10_w": _L0_conv_in["p10_w"],
    }

def reference(x, L0_conv_p1_w, L0_conv_p7_w, L0_conv_p10_w):
    import jax
    import jax.numpy as jnp
    def _L0_conv_ref(x, p1_w, p7_w, p10_w):
        import math
        import jax, jax.numpy as jnp
        import numpy as np

        def _unfold(x, kh, kw, dh, dw, ph, pw):
            n, c, h, w = x.shape
            xp = jnp.pad(x, ((0, 0), (0, 0), (ph, ph), (pw, pw)))
            patches = jnp.stack([xp[:, :, i * dh:i * dh + h, j * dw:j * dw + w] for i in range(kh) for j in range(kw)], axis=2)
            return patches
        n, c, h, w = x.shape
        g = 4
        t1 = p1_w * x
        t2 = x + t1
        t4 = jax.nn.relu(x)
        t5 = _unfold(x, 3, 7, 1, 1, 1, 3)
        t7 = jnp.einsum('oc,nchw->nohw', p7_w, t4)
        t8 = _unfold(t7, 1, 5, 1, 3, 0, 6)
        t9 = x[:, :, None] - t8
        xg = t2.reshape(n, g, c // g, h, w)
        wg = p10_w.reshape(g, c * 21 // g, c // g)
        t10 = jnp.einsum('ngihw,goi->ngohw', xg, wg).reshape(n, c * 21, h, w)
        t1f = t1.reshape(n, c, h * w)
        t5f = t5.reshape(n, c * 21, h * w)
        t11 = jnp.einsum('nck,nmk->ncm', t1f, t5f) / math.sqrt(h * w)
        t12 = t9.mean(2)
        t13 = jnp.einsum('ncm,nmk->nck', t11, t10.reshape(n, c * 21, h * w))
        t13 = t13.reshape(n, c, h, w) / math.sqrt(c * 21)
        return jnp.maximum(t13, t12)

    def _gn(v, G=32, eps=1e-5):
        B_, C_, H_, W_ = v.shape
        g = v.reshape(B_, G, C_ // G, H_, W_)
        m = jnp.mean(g, axis=(2, 3, 4), keepdims=True)
        s = jnp.var(g, axis=(2, 3, 4), keepdims=True)
        return ((g - m) / jnp.sqrt(s + eps)).reshape(v.shape)

    def _ln_c(v, eps=1e-6):
        m = jnp.mean(v, axis=1, keepdims=True)
        s = jnp.var(v, axis=1, keepdims=True)
        return (v - m) / jnp.sqrt(s + eps)

    def _ln_t(v, eps=1e-5):
        m = jnp.mean(v, axis=-1, keepdims=True)
        s = jnp.var(v, axis=-1, keepdims=True)
        return (v - m) / jnp.sqrt(s + eps)

    def _to_tokens(v):
        B_, C_, H_, W_ = v.shape
        return v.reshape(B_, C_, H_ * W_).transpose(0, 2, 1)
    def _from_tokens(t, like):
        B_, C_, H_, W_ = like.shape
        return t.transpose(0, 2, 1).reshape(B_, C_, H_, W_)

    x = _L0_conv_ref(x, L0_conv_p1_w, L0_conv_p7_w, L0_conv_p10_w)
    return x


_drawn_inputs = setup_inputs


def setup_inputs(seed=0):
    import zlib

    import numpy as np

    out = dict(_drawn_inputs(seed))
    spreads = {}
    factors = {}
    for name, (base, spread) in spreads.items():
        noise = np.random.default_rng([zlib.crc32(name.encode()), seed]).standard_normal(out[name].shape)
        drawn = base * np.exp(spread * noise) if base else spread * noise
        out[name] = jnp.asarray(drawn.astype(out[name].dtype))
    for name, factor in factors.items():
        out[name] = (out[name] * factor).astype(out[name].dtype)
    return out
```

```python
from contextlib import ExitStack

import concourse.bass as bass
from concourse import mybir

P = 128
N_IMG, C, H, W = 8, 128, 64, 64
GROUPS = 4
CG = C // GROUPS
KH, KW = 3, 7
TAPS = KH * KW
PIX = H * W
HALF = 512
ROWS, COLS = 16, 32
UNITS = 8
FS = 4
BH, BW = 33, 35
XG = BH * BW
JH, JW = 2, 4
LO, RB_W = 3, 38
PS_W = 35
SCALE = 1.0 / ((H * W) ** 0.5 * (C * TAPS) ** 0.5)
FIFTH = -1.0 / 5.0

F32 = mybir.dt.float32
F32R = mybir.dt.float32r
ALU = mybir.AluOpType
ACT = mybir.ActivationFunctionType

EXTRAS = {
    0: [],
    1: [("T", 0)],
    2: [("T", 1), ("F", 0)],
    3: [("T", 2), ("F", 1)],
    4: [("T", 3), ("F", 2)],
    5: [("T", 4), ("F", 3)],
    6: [("F", 4), ("T", 5), ("F", 5)],
    7: [("T", 6), ("F", 6), ("T", 7), ("F", 7)],
}


def conv_seq_kernel(nc, x_nat, x_conv, p1, p7T, p10, ident_in, out):
    with ExitStack() as ctx:
        def sb(name, shape, dt=F32):
            return ctx.enter_context(nc.sbuf_tensor(name, shape, dt))

        def psum(name, shape):
            return ctx.enter_context(nc.psum_tensor(name, shape, F32))

        def sem(name):
            return ctx.enter_context(nc.semaphore(name))

        conv_w_hi = sb("conv_w_hi", [P, GROUPS, JH, JW, P], F32R)
        conv_w_lo = sb("conv_w_lo", [P, GROUPS, JH, JW, P], F32R)
        p7_raw = sb("p7_raw", [P, P])
        p7_hi = sb("p7_hi", [P, P], F32R)
        p7_lo = sb("p7_lo", [P, P], F32R)
        ident = sb("ident", [P, P])
        p1_sb = sb("p1_sb", [P, H])
        p1_plus = sb("p1_plus", [P, H])
        xg_raw = sb("xg_raw", [P, 2, XG])
        xg_hi = sb("xg_hi", [P, 2, XG], F32R)
        xg_lo = sb("xg_lo", [P, 2, XG], F32R)
        xn = sb("xn", [P, 2, FS, 2 * HALF])
        t1 = sb("t1", [P, 2, HALF])
        t1T = sb("t1T", [P, 2, 4, 4, 2, P], F32R)
        y_sb = sb("y_sb", [P, 2, HALF])
        yT_hi = sb("yT_hi", [P, 2, 4, 4, GROUPS * CG], F32R)
        yT_lo = sb("yT_lo", [P, 2, 4, 4, GROUPS * CG], F32R)
        a_cross = sb("a_cross", [P, P])
        aT = sb("aT", [P, P])
        aT_hi = sb("aT_hi", [P, P], F32R)
        aT_lo = sb("aT_lo", [P, P], F32R)
        relu_pad = sb("relu_pad", [P, 2, ROWS, RB_W])
        pair_sum = sb("pair_sum", [P, 2, ROWS, PS_W])
        box = sb("box", [P, 2, ROWS, COLS])
        box_hi = sb("box_hi", [P, 2, HALF], F32R)
        box_lo = sb("box_lo", [P, 2, HALF], F32R)
        t2 = sb("t2", [P, 2, HALF])
        t2_hi = sb("t2_hi", [P, 2, HALF], F32R)
        t2_lo = sb("t2_lo", [P, 2, HALF], F32R)
        out_sb = sb("out_sb", [P, 2, HALF])

        w_raw = xn[:, 1, :, :].rearrange("p f k -> p (f k)")[:, 0:GROUPS * TAPS * CG]
        w_hi = yT_hi[:].rearrange("p q t r m -> p (q t r m)")[:, 0:GROUPS * TAPS * CG]
        w_lo = yT_lo[:].rearrange("p q t r m -> p (q t r m)")[:, 0:GROUPS * TAPS * CG]

        ps_conv = psum("ps_conv", [P, 2, HALF])
        ps_y = psum("ps_y", [P, HALF])
        ps_t = psum("ps_t", [P, HALF])
        ps_p7 = psum("ps_p7", [P, 2, HALF])
        ps_t13 = psum("ps_t13", [P, 2, HALF])
        ps_a = ps_p7[:, 0, 0:2 * P]

        w_loaded = sem("w_loaded")
        small_loaded = sem("small_loaded")
        xg_loaded = [sem(f"xg_loaded{i}") for i in range(2)]
        xn_loaded = [[sem(f"xn_loaded{p}{f}") for f in range(FS)] for p in range(2)]
        w_zeroed = sem("w_zeroed")
        w_hi_ready = sem("w_hi_ready")
        w_lo_ready = sem("w_lo_ready")
        w_placed = sem("w_placed")
        p1_plus_ready = sem("p1_plus_ready")
        p7h_ready = sem("p7h_ready")
        p7l_ready = sem("p7l_ready")
        relu_zeroed = sem("relu_zeroed")
        xh_ready = sem("xh_ready")
        xl_ready = sem("xl_ready")
        conv_done = sem("conv_done")
        y_copied = sem("y_copied")
        ytr_done = sem("ytr_done")
        yth_ready = sem("yth_ready")
        ytl_ready = sem("ytl_ready")
        t1_ready = sem("t1_ready")
        ttr_done = sem("ttr_done")
        tth_ready = sem("tth_ready")
        ttl_ready = sem("ttl_ready")
        a_done = sem("a_done")
        a_cross_ready = sem("a_cross_ready")
        aT_steps = sem("aT_steps")
        relu_ready = sem("relu_ready")
        box_steps = sem("box_steps")
        boxh_ready = sem("boxh_ready")
        boxl_ready = sem("boxl_ready")
        t2_ready = sem("t2_ready")
        t2h_ready = sem("t2h_ready")
        t2l_ready = sem("t2l_ready")
        p7_done = sem("p7_done")
        t13_done = sem("t13_done")
        base_ready = sem("base_ready")
        out_ready = sem("out_ready")
        stored = [sem(f"stored{i}") for i in range(2)]

        AT_STEPS = 3
        BOX_STEPS = 4
        W_PLACE_ENGINES = 3

        def wait(eng, s, value):
            if not (isinstance(value, int) and value <= 0):
                eng.wait_ge(s, value)

        def images(eng, run):
            run(0, 0, 0, True, False)
            with eng.Fori(0, (N_IMG - 2) // 2) as i:
                run(2 * i + 1, i, 1, True, True)
                run(2 * i + 2, i + 1, 0, True, True)
            run(N_IMG - 1, (N_IMG - 1) // 2, 1, True, True)
            run(N_IMG, N_IMG // 2, 0, False, True)

        block = ctx.enter_context(nc.Block())

        @block.sync
        def _(sp):
            def load_group(n, kk, g):
                wait(sp, xh_ready, 4 * n + g - 1)
                wait(sp, xl_ready, 4 * n + g - 1)
                sp.dma_start(xg_raw[:, g % 2, :], x_conv[n, g, :, :]).then_inc(xg_loaded[g % 2], 16)

            def load_chunk(n, par, f, before):
                if before is not None:
                    sp.wait_ge(out_ready, 8 * before + 2 * f + 2)
                sp.dma_start(xn[:, par, f, :], x_nat[n, :, f, :]).then_inc(xn_loaded[par][f], 16)

            def store(n, h):
                wait(sp, out_ready, 8 * n + h + 1)
                sp.dma_start(out[n, :, h // 2, (h % 2) * HALF:(h % 2 + 1) * HALF],
                             out_sb[:, h % 2, :]).then_inc(stored[h % 2], 16)

            for s in stored:
                sp.sem_inc(s, 16)
            w_src = p10.rearrange("(g c t) i -> c g (t i)", g=GROUPS, t=TAPS)
            for b in range(4):
                sp.dma_start(w_raw[CG * b:CG * (b + 1), :].rearrange("p (g m) -> p g m", g=GROUPS),
                             w_src).then_inc(w_loaded, 16)
            load_group(0, 0, 0)
            sp.dma_start(p1_sb[:], p1).then_inc(small_loaded, 16)
            sp.dma_start(ident[:], ident_in).then_inc(small_loaded, 16)
            sp.dma_start(p7_raw[:], p7T).then_inc(small_loaded, 16)
            load_group(0, 0, 1)
            for f in range(FS):
                load_chunk(0, 0, f, None)

            def image(n, k, par, conv, fin):
                more = not isinstance(n, int) or n < N_IMG - 1
                if isinstance(n, int) and n == 0:
                    wait(sp, w_hi_ready, 1)
                    wait(sp, w_lo_ready, 1)
                if conv:
                    load_group(n, 0, 2)
                    load_group(n, 0, 3)
                if more:
                    load_group(n + 1, 0, 0)
                if fin:
                    store(n - 1, 0)
                if more:
                    load_group(n + 1, 0, 1)
                if fin:
                    store(n - 1, 1)
                for f in range(FS):
                    if more:
                        load_chunk(n + 1, 1 - par, f, n - 1 if fin else None)
                    if fin and f < FS - 1:
                        store(n - 1, 2 * f + 2)
                        store(n - 1, 2 * f + 3)

            images(sp, image)
            for s in stored:
                sp.wait_ge(s, 16 * 4 * N_IMG + 16)

        @block.gpsimd
        def _(pool):
            nc.gpsimd.memset(conv_w_hi[:].bitcast(F32), 0.0).then_inc(w_zeroed, 1)
            nc.gpsimd.memset(conv_w_lo[:].bitcast(F32), 0.0).then_inc(w_zeroed, 1)
            nc.gpsimd.memset(relu_pad[:], 0.0).then_inc(relu_zeroed, 1)

            def by_rows(src, f):
                return src[:, ROWS * f:ROWS * (f + 1)].unsqueeze(2).broadcast_to([P, ROWS, COLS])

            def half_of(par, h):
                return xn[:, par, h // 2, (h % 2) * HALF:(h % 2 + 1) * HALF].rearrange("p (a b) -> p a b", a=ROWS)

            def t1_half(n, k, par, h):
                wait(pool, ttr_done, 8 * n + h - 1)
                pool.wait_ge(xn_loaded[par][h // 2], 16 * k + 16)
                nc.gpsimd.tensor_tensor(t1[:, h % 2, :].rearrange("p (a b) -> p a b", a=ROWS),
                                        half_of(par, h), by_rows(p1_sb, h // 2), ALU.mult).then_inc(t1_ready, 1)

            def t2_half(m, par, h):
                if h >= 2:
                    pool.wait_ge(t2h_ready, 8 * m + h - 1)
                    pool.wait_ge(t2l_ready, 8 * m + h - 1)
                else:
                    pool.wait_ge(ytr_done, 8 * m + 8)
                nc.gpsimd.tensor_tensor(t2[:, h % 2, :].rearrange("p (a b) -> p a b", a=ROWS),
                                        half_of(par, h), by_rows(p1_plus, h // 2), ALU.mult).then_inc(t2_ready, 1)

            pool.wait_ge(small_loaded, 48)
            pool.wait_ge(p1_plus_ready, 1)

            def image(n, k, par, conv, fin):
                for kind, h in (("t2", 0), ("t2", 1), ("t1", 0), ("t1", 1), ("t1", 2), ("t2", 2), ("t1", 3),
                                ("t2", 3), ("t1", 4), ("t2", 4), ("t1", 5), ("t2", 5), ("t1", 6), ("t2", 6),
                                ("t1", 7), ("t2", 7)):
                    if kind == "t1" and conv:
                        t1_half(n, k, par, h)
                    if kind == "t2" and fin:
                        t2_half(n - 1, 1 - par, h)

            images(pool, image)

        @block.scalar
        def _(act):
            def copy(dst, src):
                return nc.scalar.activation(dst, src, ACT.Copy)

            def split_group(n, s, kk):
                act.wait_ge(xg_loaded[s], 16 * kk + 16)
                copy(xg_hi[:, s, :], xg_raw[:, s, :]).then_inc(xh_ready, 1)

            def relu(m, k, par, f):
                if f:
                    act.wait_ge(box_steps, BOX_STEPS * (4 * m + f))
                act.wait_ge(xn_loaded[par][f], 16 * k + 16)
                nc.scalar.activation(relu_pad[:, :, :, LO:LO + COLS],
                                     xn[:, par, f, :].rearrange("p (w a b) -> p w a b", w=2, a=ROWS),
                                     ACT.Relu).then_inc(relu_ready, 1)

            def prepare(m, h):
                if h >= 2:
                    act.wait_ge(t13_done, 8 * m + h - 1)
                act.wait_ge(box_steps, BOX_STEPS * (4 * m + h // 2 + 1))
                copy(box_hi[:, h % 2, :], box[:, h % 2, :, :].rearrange("p a b -> p (a b)")).then_inc(boxh_ready, 1)
                act.wait_ge(t2_ready, 8 * m + h + 1)
                copy(t2_hi[:, h % 2, :], t2[:, h % 2, :]).then_inc(t2h_ready, 1)

            def y_high(idx, u):
                wait(act, ytr_done, idx + 1)
                copy(yT_hi[:, u % 2, :, :, CG * (u // 2):CG * (u // 2 + 1)],
                     ps_y[:].rearrange("p (t r i) -> p t r i", t=4, r=4)).then_inc(yth_ready, 1)

            act.wait_ge(w_loaded, 64)
            copy(w_hi, w_raw).then_inc(w_hi_ready, 1)
            act.wait_ge(small_loaded, 48)
            copy(p7_hi[:], p7_raw[:]).then_inc(p7h_ready, 1)
            split_group(0, 0, 0)
            act.wait_ge(w_zeroed, 2)
            act.wait_ge(w_hi_ready, 1)
            place_blocks(nc, copy, conv_w_hi, w_hi, 0, w_placed)
            split_group(0, 1, 0)
            act.wait_ge(relu_zeroed, 1)

            def image(n, k, par, conv, fin):
                for u in range(UNITS):
                    if conv:
                        act.wait_ge(conv_done, 8 * n + u + 1)
                        wait(act, ytr_done, 8 * n + u - 1)
                        copy(y_sb[:, u % 2, :], ps_conv[:, u % 2, :]).then_inc(y_copied, 1)
                    if u == 0:
                        if fin:
                            y_high(8 * n - 1, UNITS - 1)
                            m, mk, mpar = n - 1, k - 1 + par, 1 - par
                            relu(m, mk, mpar, 0)
                            prepare(m, 0)
                            prepare(m, 1)
                            relu(m, mk, mpar, 1)
                    if u == 1 and fin:
                        act.wait_ge(a_done, n)
                        nc.scalar.activation(a_cross[:], ps_a[:, P:2 * P], ACT.Copy,
                                             scale=SCALE).then_inc(a_cross_ready, 1)
                    if u > 0 and conv:
                        y_high(8 * n + u - 1, u - 1)
                    for kind, h in EXTRAS[u]:
                        if kind == "T" and conv:
                            act.wait_ge(ttr_done, 8 * n + h + 1)
                            q, r = h // 2 % 2, h // 4 * 2 + h % 2
                            copy(t1T[:, q, :, r, 0, :],
                                 ps_t[:].rearrange("p (t c) -> p t c", t=4)).then_inc(tth_ready, 1)
                        if kind == "F" and fin and h + 2 < 8:
                            prepare(m, h + 2)
                    if u in (2, 4) and fin:
                        relu(m, mk, mpar, u // 2 + 1)
                    if u % 2 and conv:
                        g = u // 2 + 2
                        if g < GROUPS or not isinstance(n, int) or n < N_IMG - 1:
                            split_group(n, g % 2, 2 * n + g // 2)

            images(act, image)

        @block.vector
        def _(dve):
            def low(dst, exact, high):
                return nc.vector.tensor_tensor(dst, exact, high.bitcast(F32), ALU.subtract)

            def split_group(idx, s):
                dve.wait_ge(xh_ready, idx + 1)
                low(xg_lo[:, s, :], xg_raw[:, s, :], xg_hi[:, s, :]).then_inc(xl_ready, 1)

            def box_sums(m, f):
                base = BOX_STEPS * (4 * m + f)
                dve.wait_ge(relu_ready, 4 * m + f + 1)
                nc.vector.tensor_tensor(pair_sum[:, 0], relu_pad[:, 0, :, 0:PS_W],
                                        relu_pad[:, 1, :, 1:1 + PS_W], ALU.add).then_inc(box_steps, 1)
                nc.vector.tensor_tensor(pair_sum[:, 1], relu_pad[:, 1, :, 0:PS_W],
                                        relu_pad[:, 0, :, 2:2 + PS_W], ALU.add).then_inc(box_steps, 1)
                if f:
                    dve.wait_ge(boxh_ready, 8 * m + 2 * f)
                    dve.wait_ge(boxl_ready, 8 * m + 2 * f)
                dve.wait_ge(box_steps, base + 2)
                nc.vector.tensor_tensor(box[:], pair_sum[:, :, :, 0:COLS],
                                        pair_sum[:, :, :, LO:LO + COLS], ALU.add).then_inc(box_steps, 1)
                dve.wait_ge(box_steps, base + 3)
                nc.vector.tensor_tensor(box[:], box[:], relu_pad[:, :, :, 2 * LO:2 * LO + COLS],
                                        ALU.add).then_inc(box_steps, 1)

            def prepare(m, h):
                dve.wait_ge(boxh_ready, 8 * m + h + 1)
                low(box_lo[:, h % 2, :], box[:, h % 2, :, :].rearrange("p a b -> p (a b)"),
                    box_hi[:, h % 2, :]).then_inc(boxl_ready, 1)
                dve.wait_ge(t2h_ready, 8 * m + h + 1)
                low(t2_lo[:, h % 2, :], t2[:, h % 2, :], t2_hi[:, h % 2, :]).then_inc(t2l_ready, 1)

            def y_low(idx, u):
                dve.wait_ge(yth_ready, idx + 1)
                high = yT_hi[:, u % 2, :, :, CG * (u // 2):CG * (u // 2 + 1)]
                low(yT_lo[:, u % 2, :, :, CG * (u // 2):CG * (u // 2 + 1)],
                    ps_y[:].rearrange("p (t r i) -> p t r i", t=4, r=4), high).then_inc(ytl_ready, 1)

            def output_half(m, h, par):
                dve.wait_ge(p7_done, 8 * m + h + 1)
                dve.wait_ge(stored[h % 2], 16 * (4 * m + h // 2) + 16)
                nc.vector.scalar_tensor_tensor(
                    out=out_sb[:, h % 2, :], in0=ps_p7[:, h % 2, :], scalar=FIFTH,
                    in1=xn[:, par, h // 2, (h % 2) * HALF:(h % 2 + 1) * HALF],
                    op0=ALU.mult, op1=ALU.add).then_inc(base_ready, 1)
                dve.wait_ge(t13_done, 8 * m + h + 1)
                dve.wait_ge(base_ready, 8 * m + h + 1)
                nc.vector.tensor_tensor(out_sb[:, h % 2, :], ps_t13[:, h % 2, :], out_sb[:, h % 2, :],
                                        ALU.max).then_inc(out_ready, 1)

            dve.wait_ge(small_loaded, 48)
            nc.vector.tensor_scalar_add(p1_plus[:], p1_sb[:], 1.0).then_inc(p1_plus_ready, 1)
            dve.wait_ge(w_hi_ready, 1)
            low(w_lo, w_raw, w_hi).then_inc(w_lo_ready, 1)
            dve.wait_ge(p7h_ready, 1)
            low(p7_lo[:], p7_raw[:], p7_hi[:]).then_inc(p7l_ready, 1)
            split_group(0, 0)
            dve.wait_ge(w_zeroed, 2)
            dve.wait_ge(w_lo_ready, 1)
            place_blocks(nc, nc.vector.tensor_copy, conv_w_lo, w_lo, 0, w_placed)
            split_group(1, 1)

            def image(n, k, par, conv, fin):
                m, mpar = n - 1, 1 - par
                for u in range(UNITS):
                    if u == 0 and fin:
                        y_low(8 * n - 1, UNITS - 1)
                        box_sums(m, 0)
                        prepare(m, 0)
                        prepare(m, 1)
                    if u == 1 and fin:
                        dve.wait_ge(a_cross_ready, n)
                        nc.vector.scalar_tensor_tensor(
                            out=aT[:], in0=ps_a[:, 0:P], scalar=SCALE, in1=a_cross[:],
                            op0=ALU.mult, op1=ALU.add).then_inc(aT_steps, 1)
                        dve.wait_ge(aT_steps, AT_STEPS * m + 1)
                        nc.vector.tensor_copy(aT_hi[:], aT[:]).then_inc(aT_steps, 1)
                        dve.wait_ge(aT_steps, AT_STEPS * m + 2)
                        low(aT_lo[:], aT[:], aT_hi[:]).then_inc(aT_steps, 1)
                    if u > 0 and conv:
                        y_low(8 * n + u - 1, u - 1)
                    if u == 1 and fin:
                        box_sums(m, 1)
                    for kind, h in EXTRAS[u]:
                        if kind == "T" and conv:
                            dve.wait_ge(tth_ready, 8 * n + h + 1)
                            q, r = h // 2 % 2, h // 4 * 2 + h % 2
                            low(t1T[:, q, :, r, 1, :], ps_t[:].rearrange("p (t c) -> p t c", t=4),
                                t1T[:, q, :, r, 0, :]).then_inc(ttl_ready, 1)
                        if kind == "F" and fin:
                            output_half(m, h, mpar)
                            if h + 2 < 8:
                                prepare(m, h + 2)
                    if u in (3, 5) and fin:
                        box_sums(m, (u + 1) // 2)
                    if u % 2 and conv:
                        g = u // 2 + 2
                        if g < GROUPS or not isinstance(n, int) or n < N_IMG - 1:
                            dve.wait_ge(conv_done, 8 * n + u + 1)
                            split_group(4 * n + g, g % 2)

            images(dve, image)

        @block.tensor
        def _(pe):
            def products(dst, w_parts, x_parts, start, stop):
                (wh, wl), (xh, xl) = w_parts, x_parts
                nc.tensor.matmul(dst, wh, xh, start=start, stop=False)
                nc.tensor.matmul(dst, wh, xl, start=False, stop=False)
                return nc.tensor.matmul(dst, wl, xh, start=False, stop=stop)

            def conv_unit(n, u):
                g, q = u // 2, u % 2
                pe.wait_ge(xh_ready, 4 * n + g + 1)
                pe.wait_ge(xl_ready, 4 * n + g + 1)
                wait(pe, y_copied, 8 * n + u - 1)
                xs = [part[:, g % 2, :].rearrange("p (a b) -> p a b", a=BH) for part in (xg_hi, xg_lo)]
                for jh in range(JH):
                    for jw in range(JW):
                        view = [x[:, q * ROWS + jh:q * ROWS + jh + ROWS, jw:jw + COLS] for x in xs]
                        last = products(ps_conv[:, q, :].rearrange("p (a b) -> p a b", a=ROWS),
                                        (conv_w_hi[:, g, jh, jw, :], conv_w_lo[:, g, jh, jw, :]), view,
                                        start=(jh == 0 and jw == 0), stop=(jh == JH - 1 and jw == JW - 1))
                last.then_inc(conv_done, 1)

            def transpose_y(idx, u):
                pe.wait_ge(y_copied, idx + 1)
                wait(pe, ytl_ready, idx)
                wait(pe, yth_ready, idx)
                for t in range(4):
                    last = nc.tensor.transpose(ps_y[:, P * t:P * (t + 1)],
                                               y_sb[:, u % 2, P * t:P * (t + 1)], ident[:])
                last.then_inc(ytr_done, 1)

            def transpose_t1(idx, h):
                pe.wait_ge(t1_ready, idx + 1)
                wait(pe, ttl_ready, idx)
                wait(pe, tth_ready, idx)
                for t in range(4):
                    last = nc.tensor.transpose(ps_t[:, P * t:P * (t + 1)],
                                               t1[:, h % 2, P * t:P * (t + 1)], ident[:])
                last.then_inc(ttr_done, 1)

            def y_times_t1(m):
                pe.wait_ge(yth_ready, 8 * m + 8)
                pe.wait_ge(ytl_ready, 8 * m + 8)
                pe.wait_ge(tth_ready, 8 * m + 8)
                pe.wait_ge(ttl_ready, 8 * m + 8)
                tiles = [(q, t, r) for q in range(2) for t in range(4) for r in range(4)]
                for i, (q, t, r) in enumerate(tiles):
                    nc.tensor.matmul(ps_a[:, :], yT_hi[:, q, t, r, :],
                                     t1T[:, q, t, r, :, :].rearrange("p s c -> p (s c)"),
                                     start=(i == 0), stop=False)
                    last = nc.tensor.matmul(ps_a[:, P:2 * P], yT_lo[:, q, t, r, :], t1T[:, q, t, r, 0, :],
                                            start=False, stop=(i == len(tiles) - 1))
                last.then_inc(a_done, 1)

            def output_half(m, h):
                s = h % 2
                pe.wait_ge(boxh_ready, 8 * m + h + 1)
                pe.wait_ge(boxl_ready, 8 * m + h + 1)
                if h >= 2:
                    pe.wait_ge(out_ready, 8 * m + h - 1)
                pe.wait_ge(aT_steps, AT_STEPS * m + AT_STEPS)
                products(ps_p7[:, s, :], (p7_hi[:], p7_lo[:]), (box_hi[:, s, :], box_lo[:, s, :]),
                         True, True).then_inc(p7_done, 1)
                pe.wait_ge(t2h_ready, 8 * m + h + 1)
                pe.wait_ge(t2l_ready, 8 * m + h + 1)
                products(ps_t13[:, s, :], (aT_hi[:], aT_lo[:]), (t2_hi[:, s, :], t2_lo[:, s, :]),
                         True, True).then_inc(t13_done, 1)

            pe.wait_ge(w_placed, 2)
            pe.wait_ge(p7h_ready, 1)
            pe.wait_ge(p7l_ready, 1)
            pe.wait_ge(small_loaded, 48)

            def image(n, k, par, conv, fin):
                for u in range(UNITS):
                    if conv:
                        conv_unit(n, u)
                    if u == 0 and fin:
                        transpose_y(8 * n - 1, UNITS - 1)
                    if u == 1 and fin:
                        y_times_t1(n - 1)
                    if u > 0 and conv:
                        transpose_y(8 * n + u - 1, u - 1)
                    for kind, h in EXTRAS[u]:
                        if kind == "T" and conv:
                            transpose_t1(8 * n + h, h)
                        if kind == "F" and fin:
                            output_half(n - 1, h)

            images(pe, image)


def place_blocks(nc, copy, blocks, taps, first, done):
    src = taps.rearrange("p (g t i) -> p g t i", g=GROUPS, t=TAPS)
    last = None
    for b in range(4):
        u, v = b // 2, b % 2
        for r in range(4):
            rh, rw = r // 2, r % 2
            js = [j for j in range(JW) if 0 <= 2 * j + v - rw < KW]
            for jh in range(JH):
                dh = 2 * jh + u - rh
                if not 0 <= dh < KH:
                    continue
                lo = KW * dh + 2 * js[0] + v - rw
                last = copy(blocks[CG * b:CG * (b + 1), :, jh, js[0]:js[-1] + 1, CG * r:CG * (r + 1)],
                            src[CG * b:CG * (b + 1), :, lo:lo + 2 * len(js) - 1:2, :])
    last.then_inc(done, 1)


def kernel(**inputs):
    import numpy as np
    import concourse.bacc as bacc
    from concourse.bass_utils import run_bass_kernel_spmd

    x = np.asarray(inputs["x"])
    p1 = np.asarray(inputs["L0_conv_p1_w"])
    p7 = np.asarray(inputs["L0_conv_p7_w"])
    p10 = np.asarray(inputs["L0_conv_p10_w"])
    x_nat = np.ascontiguousarray(
        x.reshape(N_IMG, C, 2, ROWS, 2, COLS, 2).transpose(0, 1, 4, 2, 6, 3, 5)).reshape(N_IMG, C, FS, 2 * HALF)
    xp = np.pad(x, ((0, 0), (0, 0), (1, 1), (3, 3)))
    x_conv = np.ascontiguousarray(
        xp.reshape(N_IMG, GROUPS, CG, BH, 2, BW, 2).transpose(0, 1, 4, 6, 2, 3, 5)).reshape(N_IMG, GROUPS, P, XG)
    arrays = {
        "x_nat": x_nat,
        "x_conv": x_conv,
        "p1": np.ascontiguousarray(p1.reshape(C, H // 2, 2).transpose(0, 2, 1)).reshape(C, H),
        "p7T": np.ascontiguousarray(p7.T),
        "p10": np.ascontiguousarray(p10),
        "identity": np.eye(P, dtype=np.float32),
    }
    nc = bacc.Bacc("TRN2", target_bir_lowering=False, num_devices=1)
    args = [nc.dram_tensor(name, a.shape, F32, kind="ExternalInput").ap() for name, a in arrays.items()]
    out = nc.dram_tensor("out", (N_IMG, C, FS, 2 * HALF), F32, kind="ExternalOutput").ap()
    conv_seq_kernel(nc, *args, out)
    result = run_bass_kernel_spmd(nc, [arrays], core_ids=[0]).results[0]["out"]
    return np.ascontiguousarray(
        result.reshape(N_IMG, C, 2, 2, 2, ROWS, COLS).transpose(0, 1, 3, 5, 2, 6, 4)).reshape(N_IMG, C, H, W)
```

```python
from contextlib import ExitStack

import concourse.bass as bass
from concourse import mybir

P = 128
N_IMG, C, H, W = 8, 128, 64, 64
GROUPS = 4
CG = C // GROUPS
KH, KW = 3, 7
TAPS = KH * KW
PIX = H * W
HALF = 512
ROWS, COLS = 16, 32
UNITS = 8
FS = 4
BH, BW = 33, 35
XG = BH * BW
JH, JW = 2, 4
LO, RB_W = 3, 38
PS_W = 35
SCALE = 1.0 / ((H * W) ** 0.5 * (C * TAPS) ** 0.5)
FIFTH = -1.0 / 5.0

F32 = mybir.dt.float32
F32R = mybir.dt.float32r
ALU = mybir.AluOpType
ACT = mybir.ActivationFunctionType

EXTRAS = {
    0: [],
    1: [("T", 0)],
    2: [("T", 1), ("F", 0)],
    3: [("T", 2), ("F", 1)],
    4: [("T", 3), ("F", 2)],
    5: [("T", 4), ("F", 3)],
    6: [("F", 4), ("T", 5), ("F", 5)],
    7: [("T", 6), ("F", 6), ("T", 7), ("F", 7)],
}


def conv_seq_kernel(nc, x_nat, x_pix, x_conv, p1, p1T, p7T, p10, ident_in, out):
    with ExitStack() as ctx:
        def sb(name, shape, dt=F32):
            return ctx.enter_context(nc.sbuf_tensor(name, shape, dt))

        def psum(name, shape):
            return ctx.enter_context(nc.psum_tensor(name, shape, F32))

        def sem(name):
            return ctx.enter_context(nc.semaphore(name))

        conv_w_hi = sb("conv_w_hi", [P, GROUPS, JH, JW, P], F32R)
        conv_w_lo = sb("conv_w_lo", [P, GROUPS, JH, JW, P], F32R)
        p7_raw = sb("p7_raw", [P, P])
        p7_hi = sb("p7_hi", [P, P], F32R)
        p7_lo = sb("p7_lo", [P, P], F32R)
        ident = sb("ident", [P, P])
        p1_sb = sb("p1_sb", [P, H])
        p1_plus = sb("p1_plus", [P, H])
        xg_raw = sb("xg_raw", [P, 2, XG])
        xg_hi = sb("xg_hi", [P, 2, XG], F32R)
        xg_lo = sb("xg_lo", [P, 2, XG], F32R)
        xn = sb("xn", [P, FS, 2 * HALF])
        xT = sb("xT", [P, 2, 2 * HALF])
        p1T_sb = sb("p1T_sb", [P, FS, HALF])
        t1f = sb("t1f", [P, 2, HALF])
        t1T = sb("t1T", [P, 2, 4, 4, 2, P], F32R)
        y_sb = sb("y_sb", [P, 2, HALF])
        yT_hi = sb("yT_hi", [P, 2, 4, 4, GROUPS * CG], F32R)
        yT_lo = sb("yT_lo", [P, 2, 4, 4, GROUPS * CG], F32R)
        a_cross = sb("a_cross", [P, P])
        aT = sb("aT", [P, P])
        aT_hi = sb("aT_hi", [P, P], F32R)
        aT_lo = sb("aT_lo", [P, P], F32R)
        relu_pad = sb("relu_pad", [P, 2, ROWS, RB_W])
        pair_sum = sb("pair_sum", [P, 2, ROWS, PS_W])
        box = sb("box", [P, 2, ROWS, COLS])
        box_hi = sb("box_hi", [P, 2, HALF], F32R)
        box_lo = sb("box_lo", [P, 2, HALF], F32R)
        t2 = sb("t2", [P, 2, HALF])
        t2_hi = sb("t2_hi", [P, 2, HALF], F32R)
        t2_lo = sb("t2_lo", [P, 2, HALF], F32R)
        out_sb = sb("out_sb", [P, 2, HALF])

        w_raw = xn[:].rearrange("p f k -> p (f k)")[:, 0:GROUPS * TAPS * CG]
        w_hi = yT_hi[:].rearrange("p q t r m -> p (q t r m)")[:, 0:GROUPS * TAPS * CG]
        w_lo = yT_lo[:].rearrange("p q t r m -> p (q t r m)")[:, 0:GROUPS * TAPS * CG]
        last_box = [xg_raw[:, 0, 0:2 * HALF], xg_raw[:, 1, 0:2 * HALF], xT[:, 0, :], xT[:, 1, :]]

        out_slots = [out_sb[:, 0, :], out_sb[:, 1, :], t1f[:, 0, :], t1f[:, 1, :]]

        def out_slot(m, h):
            return h % 4 if isinstance(m, int) and m == N_IMG - 1 else h % 2

        ps_conv = psum("ps_conv", [P, 2, HALF])
        ps_y = psum("ps_y", [P, HALF])
        ps_p7 = psum("ps_p7", [P, 2, HALF])
        ps_t13 = psum("ps_t13", [P, 2, HALF])
        ps_a = psum("ps_a", [P, 2 * P])

        w_loaded = [sem(f"w_loaded{i}") for i in range(2)]
        small_loaded = sem("small_loaded")
        xg_loaded = [sem(f"xg_loaded{i}") for i in range(2)]
        xn_loaded = [sem(f"xn_loaded{f}") for f in range(FS)]
        xT_loaded = [sem(f"xT_loaded{i}") for i in range(2)]
        w_zeroed = sem("w_zeroed")
        w_rest_zeroed = sem("w_rest_zeroed")
        w_rest_zeroed_dve = sem("w_rest_zeroed_dve")
        w_hi_ready = sem("w_hi_ready")
        w_lo_ready = sem("w_lo_ready")
        w_hi_placed = sem("w_hi_placed")
        w_hi_placed_pool = sem("w_hi_placed_pool")
        w_lo_placed = sem("w_lo_placed")
        p1_plus_ready = sem("p1_plus_ready")
        p7h_ready = sem("p7h_ready")
        p7l_ready = sem("p7l_ready")
        relu_zeroed = sem("relu_zeroed")
        xh_ready = sem("xh_ready")
        xl_ready = sem("xl_ready")
        conv_done = sem("conv_done")
        y_copied = sem("y_copied")
        ytr_done = sem("ytr_done")
        yth_ready = sem("yth_ready")
        ytl_ready = sem("ytl_ready")
        t1_ready = sem("t1_ready")
        tth_ready = sem("tth_ready")
        ttl_ready = sem("ttl_ready")
        a_done = sem("a_done")
        a_cross_ready = sem("a_cross_ready")
        aT_steps = sem("aT_steps")
        relu_ready = sem("relu_ready")
        box_steps = sem("box_steps")
        boxh_ready = sem("boxh_ready")
        boxl_ready = sem("boxl_ready")
        t2_ready = sem("t2_ready")
        t2h_ready = sem("t2h_ready")
        t2l_ready = sem("t2l_ready")
        p7_done = sem("p7_done")
        t13_done = sem("t13_done")
        base_ready = sem("base_ready")
        out_ready = sem("out_ready")
        stored = [sem(f"stored{i}") for i in range(4)]

        AT_STEPS = 3
        BOX_STEPS = 4

        def wait(eng, s, value):
            if not (isinstance(value, int) and value <= 0):
                eng.wait_ge(s, value)

        def images(eng, run):
            run(0, True, False)
            with eng.Fori(1, N_IMG - 1) as n:
                run(n, False, False)
            run(N_IMG - 1, False, True)

        LAST = N_IMG - 1
        SMALL = 16 * (3 + 4 * FS)
        BATCHES = ((0, 1), (1, GROUPS))

        def of_groups(w, batch):
            return w[:, batch[0] * TAPS * CG:batch[1] * TAPS * CG]

        block = ctx.enter_context(nc.Block())

        @block.sync
        def _(sp):
            def load_group(n, g):
                wait(sp, xh_ready, 4 * n + g - 1)
                wait(sp, xl_ready, 4 * n + g - 1)
                sp.dma_start(xg_raw[:, g % 2, :], x_conv[n, g, :, :]).then_inc(xg_loaded[g % 2], 16)

            def load_chunk(n, f):
                sp.dma_start(xn[:, f, :], x_nat[n, :, f, :]).then_inc(xn_loaded[f], 16)

            def load_pixels(n, f):
                wait(sp, t1_ready, 8 * n + 2 * f - 2)
                sp.dma_start(xT[:, f % 2, :], x_pix[n, f, :, :]).then_inc(xT_loaded[f % 2], 16)

            def store(n, h):
                sp.wait_ge(out_ready, 8 * n + h + 1)
                s = out_slot(n, h)
                sp.dma_start(out[n, :, h // 2, (h % 2) * HALF:(h % 2 + 1) * HALF],
                             out_slots[s]).then_inc(stored[s], 16)

            for s in stored:
                sp.sem_inc(s, 16)
            w_src = p10.rearrange("(g c t) i -> c g (t i)", g=GROUPS, t=TAPS)
            for i, (g0, g1) in enumerate(BATCHES):
                for b in range(4):
                    sp.dma_start(of_groups(w_raw[CG * b:CG * (b + 1), :], (g0, g1)).rearrange(
                        "p (g m) -> p g m", g=g1 - g0), w_src[:, g0:g1, :]).then_inc(w_loaded[i], 16)
                if i == 0:
                    load_group(0, 0)
            sp.dma_start(p1_sb[:], p1).then_inc(small_loaded, 16)
            sp.dma_start(ident[:], ident_in).then_inc(small_loaded, 16)
            sp.dma_start(p7_raw[:], p7T).then_inc(small_loaded, 16)
            for f in range(FS):
                for a in range(4):
                    rows = p1T[f, :, a, :].unsqueeze(0).broadcast_to([COLS, 4, C])
                    sp.dma_start(p1T_sb[COLS * a:COLS * (a + 1), f, :].rearrange("p (t c) -> p t c", t=4),
                                 rows).then_inc(small_loaded, 16)
            load_group(0, 1)
            load_pixels(0, 0)
            load_pixels(0, 1)

            def image(n, first, last):
                load_group(n, 2)
                load_group(n, 3)
                if first:
                    sp.wait_ge(w_hi_ready, 2)
                    sp.wait_ge(w_lo_ready, 2)
                if not last:
                    load_group(n + 1, 0)
                load_pixels(n, 2)
                if not first:
                    store(n - 1, 0)
                if not last:
                    load_group(n + 1, 1)
                load_pixels(n, 3)
                for f in range(FS):
                    if not first:
                        store(n - 1, 2 * f + 1)
                    load_chunk(n, f)
                    if not first and f < FS - 1:
                        store(n - 1, 2 * f + 2)
                    if not last and f in (1, 2):
                        load_pixels(n + 1, f - 1)

            images(sp, image)
            for h in range(8):
                store(LAST, h)
            for i, s in enumerate(stored):
                sp.wait_ge(s, 16 * ((4 * LAST if i < 2 else 0) + 2) + 16)

        @block.gpsimd
        def _(pool):
            for blocks in (conv_w_hi, conv_w_lo):
                nc.gpsimd.memset(blocks[:, 0:1].bitcast(F32), 0.0).then_inc(w_zeroed, 1)
            nc.gpsimd.memset(conv_w_lo[:, 1:].bitcast(F32), 0.0).then_inc(w_rest_zeroed, 1)
            pool.wait_ge(w_zeroed, 2)
            pool.wait_ge(w_rest_zeroed, 1)
            for i, batch in enumerate(BATCHES):
                pool.wait_ge(w_hi_ready, i + 1)
                if i:
                    pool.wait_ge(w_rest_zeroed_dve, 1)
                place_blocks(nc.gpsimd.tensor_copy, conv_w_hi, w_hi, (3,), batch, w_hi_placed_pool)
                pool.wait_ge(w_hi_placed_pool, i + 1)

            def t1_half(n, h):
                f = h // 2
                wait(pool, tth_ready, 8 * n + h - 1)
                wait(pool, ttl_ready, 8 * n + h - 1)
                pool.wait_ge(xT_loaded[f % 2], 16 * (2 * n + f // 2) + 16)
                nc.gpsimd.tensor_tensor(t1f[:, h % 2, :], xT[:, f % 2, (h % 2) * HALF:(h % 2 + 1) * HALF],
                                        p1T_sb[:, f, :], ALU.mult).then_inc(t1_ready, 1)

            def t2_half(m, h, last=False):
                if last:
                    pool.wait_ge(t13_done, 8 * m + h - 1)
                elif h >= 2:
                    pool.wait_ge(t2h_ready, 8 * m + h - 1)
                    pool.wait_ge(t2l_ready, 8 * m + h - 1)
                else:
                    pool.wait_ge(ytr_done, 8 * m + 8)
                pool.wait_ge(xn_loaded[h // 2], 16 * m + 16)
                factor = p1_plus[:, ROWS * (h // 2):ROWS * (h // 2 + 1)].unsqueeze(2).broadcast_to([P, ROWS, COLS])
                x_half = xn[:, h // 2, (h % 2) * HALF:(h % 2 + 1) * HALF].rearrange("p (a b) -> p a b", a=ROWS)
                nc.gpsimd.tensor_tensor(t2[:, h % 2, :].rearrange("p (a b) -> p a b", a=ROWS),
                                        x_half, factor, ALU.mult).then_inc(t2_ready, 1)

            pool.wait_ge(small_loaded, SMALL)
            pool.wait_ge(p1_plus_ready, 1)

            def image(n, first, last):
                for kind, h in (("t2", 0), ("t1", 0), ("t2", 1), ("t1", 1), ("t1", 2), ("t2", 2), ("t1", 3),
                                ("t2", 3), ("t1", 4), ("t2", 4), ("t1", 5), ("t2", 5), ("t1", 6), ("t2", 6),
                                ("t1", 7), ("t2", 7)):
                    if kind == "t1":
                        t1_half(n, h)
                    elif not first:
                        t2_half(n - 1, h)

            images(pool, image)
            pool.wait_ge(t2h_ready, 8 * LAST)
            pool.wait_ge(t2l_ready, 8 * LAST)
            for h in range(8):
                t2_half(LAST, h, last=True)

        @block.scalar
        def _(act):
            def copy(dst, src):
                return nc.scalar.activation(dst, src, ACT.Copy)

            def split_group(s, loads):
                act.wait_ge(xg_loaded[s], 16 * loads)
                copy(xg_hi[:, s, :], xg_raw[:, s, :]).then_inc(xh_ready, 1)

            def relu(m, f):
                if f:
                    act.wait_ge(box_steps, BOX_STEPS * (4 * m + f))
                act.wait_ge(xn_loaded[f], 16 * m + 16)
                nc.scalar.activation(relu_pad[:, :, :, LO:LO + COLS],
                                     xn[:, f, :].rearrange("p (w a b) -> p w a b", w=2, a=ROWS),
                                     ACT.Relu).then_inc(relu_ready, 1)

            def prepare(m, h):
                if h >= 2:
                    act.wait_ge(t13_done, 8 * m + h - 1)
                act.wait_ge(box_steps, BOX_STEPS * (4 * m + h // 2 + 1))
                copy(box_hi[:, h % 2, :], box[:, h % 2, :, :].rearrange("p a b -> p (a b)")).then_inc(boxh_ready, 1)
                act.wait_ge(t2_ready, 8 * m + h + 1)
                copy(t2_hi[:, h % 2, :], t2[:, h % 2, :]).then_inc(t2h_ready, 1)

            def y_high(idx, u):
                wait(act, ytr_done, idx + 1)
                copy(yT_hi[:, u % 2, :, :, CG * (u // 2):CG * (u // 2 + 1)],
                     ps_y[:].rearrange("p (t r i) -> p t r i", t=4, r=4)).then_inc(yth_ready, 1)

            def a_cross_part(m):
                act.wait_ge(a_done, m + 1)
                nc.scalar.activation(a_cross[:], ps_a[:, P:2 * P], ACT.Copy,
                                     scale=SCALE).then_inc(a_cross_ready, 1)

            act.wait_ge(w_loaded[0], 64)
            copy(of_groups(w_hi, BATCHES[0]), of_groups(w_raw, BATCHES[0])).then_inc(w_hi_ready, 1)
            act.wait_ge(w_zeroed, 2)
            act.wait_ge(w_hi_ready, 1)
            place_blocks(copy, conv_w_hi, w_hi, (0, 1, 2), BATCHES[0], w_hi_placed)
            split_group(0, 1)
            act.wait_ge(w_loaded[1], 64)
            copy(of_groups(w_hi, BATCHES[1]), of_groups(w_raw, BATCHES[1])).then_inc(w_hi_ready, 1)
            act.wait_ge(w_rest_zeroed_dve, 1)
            act.wait_ge(w_hi_ready, 2)
            place_blocks(copy, conv_w_hi, w_hi, (0, 1, 2), BATCHES[1], w_hi_placed)
            split_group(1, 1)
            act.wait_ge(small_loaded, SMALL)
            copy(p7_hi[:], p7_raw[:]).then_inc(p7h_ready, 1)
            act.wait_ge(relu_zeroed, 1)

            def image(n, first, last):
                m = n - 1
                for u in range(UNITS):
                    act.wait_ge(conv_done, 8 * n + u + 1)
                    wait(act, ytr_done, 8 * n + u - 1)
                    copy(y_sb[:, u % 2, :], ps_conv[:, u % 2, :]).then_inc(y_copied, 1)
                    if u == 0 and not first:
                        y_high(8 * n - 1, UNITS - 1)
                        relu(m, 0)
                        prepare(m, 0)
                        prepare(m, 1)
                        relu(m, 1)
                    if u == 1 and not first:
                        a_cross_part(m)
                    if first and u == 1:
                        act.wait_ge(w_hi_placed_pool, 2)
                    if u > 0:
                        y_high(8 * n + u - 1, u - 1)
                    for kind, h in EXTRAS[u]:
                        if kind == "T":
                            act.wait_ge(t1_ready, 8 * n + h + 1)
                            q, r = h // 2 % 2, h // 4 * 2 + h % 2
                            copy(t1T[:, q, :, r, 0, :],
                                 t1f[:, h % 2, :].rearrange("p (t c) -> p t c", t=4)).then_inc(tth_ready, 1)
                        elif not first and h + 2 < 8:
                            prepare(m, h + 2)
                    if u in (2, 4) and not first:
                        relu(m, u // 2 + 1)
                    if u in (1, 3) or (u in (5, 7) and not last):
                        g = u // 2 + 2
                        split_group(g % 2, 2 * n + g // 2 + 1)

            images(act, image)
            y_high(8 * N_IMG - 1, UNITS - 1)
            for f in range(FS):
                relu(LAST, f)
                if f == 1:
                    a_cross_part(LAST)

        @block.vector
        def _(dve):
            def low(dst, exact, high):
                return nc.vector.tensor_tensor(dst, exact, high.bitcast(F32), ALU.subtract)

            def split_group(idx, s):
                dve.wait_ge(xh_ready, idx + 1)
                low(xg_lo[:, s, :], xg_raw[:, s, :], xg_hi[:, s, :]).then_inc(xl_ready, 1)

            def box_sums(m, f, last=False):
                base = BOX_STEPS * (4 * m + f)
                dve.wait_ge(relu_ready, 4 * m + f + 1)
                nc.vector.tensor_tensor(pair_sum[:, 0], relu_pad[:, 0, :, 0:PS_W],
                                        relu_pad[:, 1, :, 1:1 + PS_W], ALU.add).then_inc(box_steps, 1)
                nc.vector.tensor_tensor(pair_sum[:, 1], relu_pad[:, 1, :, 0:PS_W],
                                        relu_pad[:, 0, :, 2:2 + PS_W], ALU.add).then_inc(box_steps, 1)
                dst = box[:]
                if last:
                    dst = last_box[f].rearrange("p (w a b) -> p w a b", w=2, a=ROWS)
                    if f >= 2:
                        dve.wait_ge(t1_ready, 8 * N_IMG)
                elif f:
                    dve.wait_ge(boxh_ready, 8 * m + 2 * f)
                    dve.wait_ge(boxl_ready, 8 * m + 2 * f)
                dve.wait_ge(box_steps, base + 2)
                nc.vector.tensor_tensor(dst, pair_sum[:, :, :, 0:COLS],
                                        pair_sum[:, :, :, LO:LO + COLS], ALU.add).then_inc(box_steps, 1)
                dve.wait_ge(box_steps, base + 3)
                nc.vector.tensor_tensor(dst, dst, relu_pad[:, :, :, 2 * LO:2 * LO + COLS],
                                        ALU.add).then_inc(box_steps, 1)

            def prepare(m, h):
                dve.wait_ge(boxh_ready, 8 * m + h + 1)
                low(box_lo[:, h % 2, :], box[:, h % 2, :, :].rearrange("p a b -> p (a b)"),
                    box_hi[:, h % 2, :]).then_inc(boxl_ready, 1)
                dve.wait_ge(t2h_ready, 8 * m + h + 1)
                low(t2_lo[:, h % 2, :], t2[:, h % 2, :], t2_hi[:, h % 2, :]).then_inc(t2l_ready, 1)

            def y_low(idx, u):
                dve.wait_ge(yth_ready, idx + 1)
                high = yT_hi[:, u % 2, :, :, CG * (u // 2):CG * (u // 2 + 1)]
                low(yT_lo[:, u % 2, :, :, CG * (u // 2):CG * (u // 2 + 1)],
                    ps_y[:].rearrange("p (t r i) -> p t r i", t=4, r=4), high).then_inc(ytl_ready, 1)

            def base_half(m, h):
                dve.wait_ge(p7_done, 8 * m + h + 1)
                s = out_slot(m, h)
                loads = 4 * m + h // 2
                if s >= 2:
                    loads = h // 4
                elif isinstance(m, int) and m == LAST and h >= 4:
                    loads = 4 * m + h // 4
                dve.wait_ge(stored[s], 16 * loads + 16)
                nc.vector.scalar_tensor_tensor(
                    out=out_slots[s], in0=ps_p7[:, h % 2, :], scalar=FIFTH,
                    in1=xn[:, h // 2, (h % 2) * HALF:(h % 2 + 1) * HALF],
                    op0=ALU.mult, op1=ALU.add).then_inc(base_ready, 1)

            def max_half(m, h):
                s = out_slot(m, h)
                dve.wait_ge(t13_done, 8 * m + h + 1)
                dve.wait_ge(base_ready, 8 * m + h + 1)
                nc.vector.tensor_tensor(out_slots[s], ps_t13[:, h % 2, :], out_slots[s],
                                        ALU.max).then_inc(out_ready, 1)

            def join_aT(m):
                dve.wait_ge(a_cross_ready, m + 1)
                nc.vector.scalar_tensor_tensor(
                    out=aT[:], in0=ps_a[:, 0:P], scalar=SCALE, in1=a_cross[:],
                    op0=ALU.mult, op1=ALU.add).then_inc(aT_steps, 1)

            nc.vector.memset(conv_w_hi[:, 1:].bitcast(F32), 0.0).then_inc(w_rest_zeroed_dve, 1)
            nc.vector.memset(relu_pad[:], 0.0).then_inc(relu_zeroed, 1)
            for i, batch in enumerate(BATCHES):
                dve.wait_ge(w_hi_ready, i + 1)
                low(of_groups(w_lo, batch), of_groups(w_raw, batch), of_groups(w_hi, batch)).then_inc(w_lo_ready, 1)
                dve.wait_ge(w_rest_zeroed if i else w_zeroed, 2 - i)
                dve.wait_ge(w_lo_ready, i + 1)
                place_blocks(nc.vector.tensor_copy, conv_w_lo, w_lo, (0, 1, 2, 3), batch, w_lo_placed)
                split_group(i, i)
            dve.wait_ge(small_loaded, SMALL)
            nc.vector.tensor_scalar_add(p1_plus[:], p1_sb[:], 1.0).then_inc(p1_plus_ready, 1)
            dve.wait_ge(p7h_ready, 1)
            low(p7_lo[:], p7_raw[:], p7_hi[:]).then_inc(p7l_ready, 1)

            def image(n, first, last):
                m = n - 1
                for u in range(UNITS):
                    if u == 0 and not first:
                        y_low(8 * n - 1, UNITS - 1)
                        box_sums(m, 0)
                        prepare(m, 0)
                        prepare(m, 1)
                    if u == 1 and not first:
                        join_aT(m)
                        dve.wait_ge(aT_steps, AT_STEPS * m + 1)
                        nc.vector.tensor_copy(aT_hi[:], aT[:]).then_inc(aT_steps, 1)
                        dve.wait_ge(aT_steps, AT_STEPS * m + 2)
                        low(aT_lo[:], aT[:], aT_hi[:]).then_inc(aT_steps, 1)
                    if u > 0:
                        y_low(8 * n + u - 1, u - 1)
                    if u == 1 and not first:
                        box_sums(m, 1)
                    for kind, h in EXTRAS[u]:
                        if kind == "T":
                            dve.wait_ge(tth_ready, 8 * n + h + 1)
                            q, r = h // 2 % 2, h // 4 * 2 + h % 2
                            low(t1T[:, q, :, r, 1, :], t1f[:, h % 2, :].rearrange("p (t c) -> p t c", t=4),
                                t1T[:, q, :, r, 0, :]).then_inc(ttl_ready, 1)
                        elif not first:
                            base_half(m, h)
                            max_half(m, h)
                            if h + 2 < 8:
                                prepare(m, h + 2)
                    if u in (3, 5) and not first:
                        box_sums(m, (u + 1) // 2)
                    if u in (1, 3) or (u in (5, 7) and not last):
                        g = u // 2 + 2
                        dve.wait_ge(conv_done, 8 * n + u + 1)
                        split_group(4 * n + g, g % 2)

            images(dve, image)
            y_low(8 * N_IMG - 1, UNITS - 1)
            box_sums(LAST, 0, last=True)
            box_sums(LAST, 1, last=True)
            join_aT(LAST)
            base_half(LAST, 0)
            base_half(LAST, 1)
            for h in range(8):
                max_half(LAST, h)
                if h in (1, 3):
                    box_sums(LAST, h // 2 + 2, last=True)
                if h + 2 < 8:
                    base_half(LAST, h + 2)

        @block.tensor
        def _(pe):
            def products(dst, w_parts, x_parts, start, stop):
                (wh, wl), (xh, xl) = w_parts, x_parts
                nc.tensor.matmul(dst, wh, xh, start=start, stop=False)
                nc.tensor.matmul(dst, wh, xl, start=False, stop=False)
                return nc.tensor.matmul(dst, wl, xh, start=False, stop=stop)

            def conv_unit(n, u):
                g, q = u // 2, u % 2
                pe.wait_ge(xh_ready, 4 * n + g + 1)
                pe.wait_ge(xl_ready, 4 * n + g + 1)
                wait(pe, y_copied, 8 * n + u - 1)
                xs = [part[:, g % 2, :].rearrange("p (a b) -> p a b", a=BH) for part in (xg_hi, xg_lo)]
                for jh in range(JH):
                    for jw in range(JW):
                        view = [x[:, q * ROWS + jh:q * ROWS + jh + ROWS, jw:jw + COLS] for x in xs]
                        last = products(ps_conv[:, q, :].rearrange("p (a b) -> p a b", a=ROWS),
                                        (conv_w_hi[:, g, jh, jw, :], conv_w_lo[:, g, jh, jw, :]), view,
                                        start=(jh == 0 and jw == 0), stop=(jh == JH - 1 and jw == JW - 1))
                last.then_inc(conv_done, 1)

            def transpose_y(idx, u):
                pe.wait_ge(y_copied, idx + 1)
                wait(pe, ytl_ready, idx)
                wait(pe, yth_ready, idx)
                for t in range(4):
                    last = nc.tensor.transpose(ps_y[:, P * t:P * (t + 1)],
                                               y_sb[:, u % 2, P * t:P * (t + 1)], ident[:])
                last.then_inc(ytr_done, 1)

            def y_times_t1(m):
                pe.wait_ge(yth_ready, 8 * m + 8)
                pe.wait_ge(ytl_ready, 8 * m + 8)
                pe.wait_ge(tth_ready, 8 * m + 8)
                pe.wait_ge(ttl_ready, 8 * m + 8)
                tiles = [(q, t, r) for q in range(2) for t in range(4) for r in range(4)]
                for i, (q, t, r) in enumerate(tiles):
                    nc.tensor.matmul(ps_a[:, :], yT_hi[:, q, t, r, :],
                                     t1T[:, q, t, r, :, :].rearrange("p s c -> p (s c)"),
                                     start=(i == 0), stop=False)
                    last = nc.tensor.matmul(ps_a[:, P:2 * P], yT_lo[:, q, t, r, :], t1T[:, q, t, r, 0, :],
                                            start=False, stop=(i == len(tiles) - 1))
                last.then_inc(a_done, 1)

            def output_half(m, h):
                s = h % 2
                pe.wait_ge(boxh_ready, 8 * m + h + 1)
                pe.wait_ge(boxl_ready, 8 * m + h + 1)
                if h >= 2:
                    pe.wait_ge(out_ready, 8 * m + h - 1)
                pe.wait_ge(aT_steps, AT_STEPS * m + AT_STEPS)
                products(ps_p7[:, s, :], (p7_hi[:], p7_lo[:]), (box_hi[:, s, :], box_lo[:, s, :]),
                         True, True).then_inc(p7_done, 1)
                pe.wait_ge(t2h_ready, 8 * m + h + 1)
                pe.wait_ge(t2l_ready, 8 * m + h + 1)
                products(ps_t13[:, s, :], (aT_hi[:], aT_lo[:]), (t2_hi[:, s, :], t2_lo[:, s, :]),
                         True, True).then_inc(t13_done, 1)

            def last_p7(h):
                pe.wait_ge(box_steps, BOX_STEPS * (4 * LAST + h // 2 + 1))
                pe.wait_ge(base_ready, 8 * LAST + h - 1)
                nc.tensor.matmul(ps_p7[:, h % 2, :], p7_raw[:], last_box[h // 2][:, (h % 2) * HALF:(h % 2 + 1) * HALF],
                                 start=True, stop=True).then_inc(p7_done, 1)

            def last_t13(h):
                pe.wait_ge(aT_steps, AT_STEPS * LAST + 1)
                pe.wait_ge(t2_ready, 8 * LAST + h + 1)
                pe.wait_ge(out_ready, 8 * LAST + h - 1)
                nc.tensor.matmul(ps_t13[:, h % 2, :], aT[:], t2[:, h % 2, :],
                                 start=True, stop=True).then_inc(t13_done, 1)

            def image(n, first, last):
                for u in range(UNITS):
                    if first and u in (0, 2):
                        pe.wait_ge(w_hi_placed, u // 2 + 1)
                        pe.wait_ge(w_hi_placed_pool, u // 2 + 1)
                        pe.wait_ge(w_lo_placed, u // 2 + 1)
                    conv_unit(n, u)
                    if first and u == 1:
                        pe.wait_ge(small_loaded, SMALL)
                        pe.wait_ge(p7h_ready, 1)
                        pe.wait_ge(p7l_ready, 1)
                    if u == 0 and not first:
                        transpose_y(8 * n - 1, UNITS - 1)
                    if u == 1 and not first:
                        y_times_t1(n - 1)
                    if u > 0:
                        transpose_y(8 * n + u - 1, u - 1)
                    for kind, h in EXTRAS[u]:
                        if kind == "F" and not first:
                            output_half(n - 1, h)

            images(pe, image)
            transpose_y(8 * N_IMG - 1, UNITS - 1)
            y_times_t1(LAST)
            last_p7(0)
            last_p7(1)
            for h in range(8):
                last_t13(h)
                if h + 2 < 8:
                    last_p7(h + 2)


def place_blocks(copy, blocks, taps, uvs, groups, done):
    src = taps.rearrange("p (g t i) -> p g t i", g=GROUPS, t=TAPS)
    g0, g1 = groups
    last = None
    for b in uvs:
        u, v = b // 2, b % 2
        for r in range(4):
            rh, rw = r // 2, r % 2
            js = [j for j in range(JW) if 0 <= 2 * j + v - rw < KW]
            for jh in range(JH):
                dh = 2 * jh + u - rh
                if not 0 <= dh < KH:
                    continue
                lo = KW * dh + 2 * js[0] + v - rw
                last = copy(blocks[CG * b:CG * (b + 1), g0:g1, jh, js[0]:js[-1] + 1, CG * r:CG * (r + 1)],
                            src[CG * b:CG * (b + 1), g0:g1, lo:lo + 2 * len(js) - 1:2, :])
    last.then_inc(done, 1)


def kernel(**inputs):
    import numpy as np
    import concourse.bacc as bacc
    from concourse.bass_utils import run_bass_kernel_spmd

    x = np.asarray(inputs["x"])
    p1 = np.asarray(inputs["L0_conv_p1_w"])
    p7 = np.asarray(inputs["L0_conv_p7_w"])
    p10 = np.asarray(inputs["L0_conv_p10_w"])
    x_nat = np.ascontiguousarray(
        x.reshape(N_IMG, C, 2, ROWS, 2, COLS, 2).transpose(0, 1, 4, 2, 6, 3, 5)).reshape(N_IMG, C, FS, 2 * HALF)
    x_pix = np.ascontiguousarray(
        x_nat.reshape(N_IMG, C, FS, 2, 4, P).transpose(0, 2, 5, 3, 4, 1)).reshape(N_IMG, FS, P, 2 * HALF)
    xp = np.pad(x, ((0, 0), (0, 0), (1, 1), (3, 3)))
    x_conv = np.ascontiguousarray(
        xp.reshape(N_IMG, GROUPS, CG, BH, 2, BW, 2).transpose(0, 1, 4, 6, 2, 3, 5)).reshape(N_IMG, GROUPS, P, XG)
    arrays = {
        "x_nat": x_nat,
        "x_pix": x_pix,
        "x_conv": x_conv,
        "p1": np.ascontiguousarray(p1.reshape(C, H // 2, 2).transpose(0, 2, 1)).reshape(C, H),
        "p1T": np.ascontiguousarray(p1.reshape(C, 2, 4, 4, 2).transpose(4, 1, 2, 3, 0)).reshape(FS, 4, 4, C),
        "p7T": np.ascontiguousarray(p7.T),
        "p10": np.ascontiguousarray(p10),
        "identity": np.eye(P, dtype=np.float32),
    }
    nc = bacc.Bacc("TRN2", target_bir_lowering=False, num_devices=1)
    args = [nc.dram_tensor(name, a.shape, F32, kind="ExternalInput").ap() for name, a in arrays.items()]
    out = nc.dram_tensor("out", (N_IMG, C, FS, 2 * HALF), F32, kind="ExternalOutput").ap()
    conv_seq_kernel(nc, *args, out)
    result = run_bass_kernel_spmd(nc, [arrays], core_ids=[0]).results[0]["out"]
    return np.ascontiguousarray(
        result.reshape(N_IMG, C, 2, 2, 2, ROWS, COLS).transpose(0, 1, 3, 5, 2, 6, 4)).reshape(N_IMG, C, H, W)
```

```python
from contextlib import ExitStack

import concourse.bass as bass
from concourse import mybir

P = 128
N_IMG, C, H, W = 8, 128, 64, 64
GROUPS = 4
CG = C // GROUPS
KH, KW = 3, 7
TAPS = KH * KW
TILES = 32
HALF = 512
ROWS, COLS = 16, 32
UNITS = 8
FS = 4
BH, BW = 33, 35
XG = BH * BW
JH, JW = 2, 4
LO, RB_W = 3, 38
PS_W = 35
SCALE = 1.0 / ((H * W) ** 0.5 * (C * TAPS) ** 0.5)
FIFTH = -1.0 / 5.0

F32 = mybir.dt.float32
F32R = mybir.dt.float32r
ALU = mybir.AluOpType
ACT = mybir.ActivationFunctionType

EXTRAS = {
    0: [],
    1: [("T", 0)],
    2: [("T", 1), ("F", 0)],
    3: [("T", 2), ("F", 1)],
    4: [("T", 3), ("F", 2)],
    5: [("T", 4), ("F", 3)],
    6: [("F", 4), ("T", 5), ("F", 5)],
    7: [("T", 6), ("F", 6), ("T", 7), ("F", 7)],
}

FIRST_F = {u: next((h for kind, h in extras if kind == "F"), 0) for u, extras in EXTRAS.items()}


def conv_seq_kernel(nc, x_nat, x_pix, x_conv, p1, p1T, p7T, p10, out):
    with ExitStack() as ctx:
        def sb(name, shape, dt=F32):
            return ctx.enter_context(nc.sbuf_tensor(name, shape, dt))

        def psum(name, shape):
            return ctx.enter_context(nc.psum_tensor(name, shape, F32))

        def sem(name):
            return ctx.enter_context(nc.semaphore(name))

        conv_w_hi = sb("conv_w_hi", [P, GROUPS, JH, JW, P], F32R)
        conv_w_lo = sb("conv_w_lo", [P, GROUPS, JH, JW, P], F32R)
        p7_raw = sb("p7_raw", [P, P])
        p7_hi = sb("p7_hi", [P, P], F32R)
        p7_lo = sb("p7_lo", [P, P], F32R)
        p1_sb = sb("p1_sb", [P, H])
        p1_plus = sb("p1_plus", [P, H])
        xg_raw = sb("xg_raw", [P, XG])
        xg_hi = sb("xg_hi", [P, 2, XG], F32R)
        xg_lo = sb("xg_lo", [P, 2, XG], F32R)
        xn = sb("xn", [P, FS, 2 * HALF])
        xT = sb("xT", [P, 2, 2 * HALF])
        p1T_sb = sb("p1T_sb", [P, TILES, C])
        t1f = sb("t1f", [P, 2, HALF])
        t1T = sb("t1T", [P, TILES, 2, C], F32R)
        yT_hi = sb("yT_hi", [P, TILES, GROUPS * CG], F32R)
        yT_lo = sb("yT_lo", [P, TILES, GROUPS * CG], F32R)
        a_cross = sb("a_cross", [P, P])
        aT = sb("aT", [P, P])
        aT_hi = sb("aT_hi", [P, P], F32R)
        aT_lo = sb("aT_lo", [P, P], F32R)
        relu_pad = sb("relu_pad", [P, 2, ROWS, RB_W])
        pair_sum = sb("pair_sum", [P, 2, ROWS, PS_W])
        box = sb("box", [P, 2, ROWS, COLS])
        box_hi = sb("box_hi", [P, 2, HALF], F32R)
        box_lo = sb("box_lo", [P, 2, HALF], F32R)
        t2 = sb("t2", [P, 2, HALF])
        t2_hi = sb("t2_hi", [P, 2, HALF], F32R)
        t2_lo = sb("t2_lo", [P, 2, HALF], F32R)
        out_sb = sb("out_sb", [P, 2, HALF])

        w_raw = xn[:].rearrange("p f k -> p (f k)")[:, 0:GROUPS * TAPS * CG]
        w_hi = yT_hi[:].rearrange("p t m -> p (t m)")[:, 0:GROUPS * TAPS * CG]
        w_lo = yT_lo[:].rearrange("p t m -> p (t m)")[:, 0:GROUPS * TAPS * CG]
        last_box = [p1T_sb[:, 8 * f:8 * f + 8, :].rearrange("p t c -> p (t c)") for f in range(FS)]

        pool_relu = xT[:].rearrange("p s k -> p (s k)")[:, 0:2 * ROWS * RB_W].rearrange(
            "p (w a b) -> p w a b", w=2, a=ROWS)
        pool_pair = xg_raw[:, 0:2 * ROWS * PS_W].rearrange("p (w a b) -> p w a b", w=2, a=ROWS)

        out_slots = [out_sb[:, 0, :], out_sb[:, 1, :], t1f[:, 0, :], t1f[:, 1, :]]

        def out_slot(m, h):
            return (h + 2) % 4 if isinstance(m, int) and m == N_IMG - 1 else h % 2

        ps_conv = psum("ps_conv", [P, 2, HALF])
        ps_yT = psum("ps_yT", [P, HALF])
        ps_p7 = psum("ps_p7", [P, 2, HALF])
        ps_t13 = psum("ps_t13", [P, 2, HALF])
        ps_a = psum("ps_a", [P, 2 * P])
        last_p7_banks = [ps_conv[:, 0, :], ps_conv[:, 1, :], ps_p7[:, 0, :], ps_p7[:, 1, :]]

        w_loaded = [sem(f"w_loaded{i}") for i in range(2)]
        small_loaded = sem("small_loaded")
        xg_loaded = sem("xg_loaded")
        xn_loaded = [sem(f"xn_loaded{f}") for f in range(FS)]
        xT_loaded = [sem(f"xT_loaded{i}") for i in range(2)]
        w_zeroed = sem("w_zeroed")
        w_rest_zeroed = sem("w_rest_zeroed")
        w_rest_zeroed_dve = sem("w_rest_zeroed_dve")
        w_hi_ready = sem("w_hi_ready")
        w_lo_ready = sem("w_lo_ready")
        w_hi_placed = sem("w_hi_placed")
        w_hi_placed_pool = sem("w_hi_placed_pool")
        w_lo_placed = sem("w_lo_placed")
        p1_plus_ready = sem("p1_plus_ready")
        p7h_ready = sem("p7h_ready")
        p7l_ready = sem("p7l_ready")
        relu_zeroed = sem("relu_zeroed")
        xh_ready = sem("xh_ready")
        xl_ready = sem("xl_ready")
        conv_done = sem("conv_done")
        y_turned = sem("y_turned")
        yth_ready = sem("yth_ready")
        ytl_ready = sem("ytl_ready")
        t1_ready = sem("t1_ready")
        tth_ready = sem("tth_ready")
        ttl_ready = sem("ttl_ready")
        a_done = sem("a_done")
        a_cross_ready = sem("a_cross_ready")
        aT_steps = sem("aT_steps")
        relu_ready = sem("relu_ready")
        box_steps = sem("box_steps")
        pool_relu_zeroed = sem("pool_relu_zeroed")
        pool_relu_ready = sem("pool_relu_ready")
        pool_box_steps = sem("pool_box_steps")
        boxh_ready = sem("boxh_ready")
        boxl_ready = sem("boxl_ready")
        t2_ready = sem("t2_ready")
        t2h_ready = sem("t2h_ready")
        t2l_ready = sem("t2l_ready")
        p7_done = sem("p7_done")
        t13_done = sem("t13_done")
        base_ready = sem("base_ready")
        out_ready = sem("out_ready")
        stored = [sem(f"stored{i}") for i in range(4)]

        AT_STEPS = 3
        BOX_STEPS = 4

        def wait(eng, s, value):
            if not (isinstance(value, int) and value <= 0):
                eng.wait_ge(s, value)

        def images(eng, run):
            run(0, True, False)
            with eng.Fori(1, N_IMG - 1) as n:
                run(n, False, False)
            run(N_IMG - 1, False, True)

        LAST = N_IMG - 1
        WARM_UP = 15
        SMALL = 16 * 4
        POOL_BOX = 1
        DVE_BOXES = [f for f in range(FS) if f != POOL_BOX]
        BATCHES = ((0, 1), (1, GROUPS))

        def of_groups(w, batch):
            return w[:, batch[0] * TAPS * CG:batch[1] * TAPS * CG]

        block = ctx.enter_context(nc.Block())

        @block.sync
        def _(sp):
            def load_group(n, g):
                wait(sp, xh_ready, 4 * n + g)
                wait(sp, xl_ready, 4 * n + g)
                sp.dma_start(xg_raw[:], x_conv[n, g, :, :]).then_inc(xg_loaded, 16)

            def load_chunk(n, f):
                sp.dma_start(xn[:, f, :], x_nat[n, :, f, :]).then_inc(xn_loaded[f], 16)

            def load_pixels(n, f):
                wait(sp, t1_ready, 8 * n + 2 * f - 2)
                sp.dma_start(xT[:, f % 2, :], x_pix[n, f, :, :]).then_inc(xT_loaded[f % 2], 16)

            def store(n, h):
                sp.wait_ge(out_ready, 8 * n + h + 1)
                s = out_slot(n, h)
                sp.dma_start(out[n, :, h // 2, (h % 2) * HALF:(h % 2 + 1) * HALF],
                             out_slots[s]).then_inc(stored[s], 16)

            for s in stored:
                sp.sem_inc(s, 16)
            w_src = p10.rearrange("(g c t) i -> c g (t i)", g=GROUPS, t=TAPS)
            for i, (g0, g1) in enumerate(BATCHES):
                for b in range(4):
                    sp.dma_start(of_groups(w_raw[CG * b:CG * (b + 1), :], (g0, g1)).rearrange(
                        "p (g m) -> p g m", g=g1 - g0), w_src[:, g0:g1, :]).then_inc(w_loaded[i], 16)
                if i == 0:
                    load_group(0, 0)
            sp.dma_start(p1_sb[:], p1).then_inc(small_loaded, 16)
            sp.dma_start(p7_raw[:], p7T).then_inc(small_loaded, 16)
            load_pixels(0, 0)
            load_group(0, 1)
            for rh in range(2):
                sp.dma_start(p1T_sb[P // 2 * rh:P // 2 * (rh + 1), :, :],
                             p1T[rh, :, :].unsqueeze(0).broadcast_to([P // 2, TILES, C])).then_inc(small_loaded, 16)
            load_pixels(0, 1)

            def image(n, first, last):
                load_group(n, 2)
                if first:
                    sp.wait_ge(w_hi_ready, 2)
                    sp.wait_ge(w_lo_ready, 2)
                load_pixels(n, 2)
                load_group(n, 3)
                if not first:
                    store(n - 1, 0)
                load_pixels(n, 3)
                for f in range(FS):
                    if not first:
                        store(n - 1, 2 * f + 1)
                    load_chunk(n, f)
                    if not last and f in (0, 2):
                        load_group(n + 1, f // 2)
                    if not first and f < FS - 1:
                        store(n - 1, 2 * f + 2)
                    if not last and f in (1, 2):
                        load_pixels(n + 1, f - 1)

            images(sp, image)
            for h in range(8):
                store(LAST, h)
            for i, s in enumerate(stored):
                sp.wait_ge(s, 16 * ((4 * LAST if i < 2 else 0) + 2) + 16)

        @block.gpsimd
        def _(pool):
            for blocks in (conv_w_hi, conv_w_lo):
                nc.gpsimd.memset(blocks[:, 0:1].bitcast(F32), 0.0).then_inc(w_zeroed, 1)
            nc.gpsimd.memset(conv_w_lo[:, 1:].bitcast(F32), 0.0).then_inc(w_rest_zeroed, 1)
            pool.wait_ge(w_zeroed, 2)
            pool.wait_ge(w_rest_zeroed, 1)
            for i, batch in enumerate(BATCHES):
                pool.wait_ge(w_hi_ready, i + 1)
                if i:
                    pool.wait_ge(w_rest_zeroed_dve, 1)
                place_blocks(nc.gpsimd.tensor_copy, conv_w_hi, w_hi, (3,), batch, w_hi_placed_pool)
                pool.wait_ge(w_hi_placed_pool, i + 1)

            def t1_half(n, h):
                f = h // 2
                wait(pool, tth_ready, 8 * n + h - 1)
                wait(pool, ttl_ready, 8 * n + h - 1)
                pool.wait_ge(xT_loaded[f % 2], 16 * (2 * n + f // 2) + 16)
                nc.gpsimd.tensor_tensor(t1f[:, h % 2, :], xT[:, f % 2, (h % 2) * HALF:(h % 2 + 1) * HALF],
                                        p1T_sb[:, 4 * h:4 * h + 4, :].rearrange("p t c -> p (t c)"),
                                        ALU.mult).then_inc(t1_ready, 1)

            def t2_half(m, h, last=False):
                if last:
                    if h >= 2:
                        pool.wait_ge(t13_done, 8 * m + h - 1)
                elif h >= 2:
                    pool.wait_ge(t2h_ready, 8 * m + h - 1)
                    pool.wait_ge(t2l_ready, 8 * m + h - 1)
                else:
                    pool.wait_ge(conv_done, 8 * m + 9)
                pool.wait_ge(xn_loaded[h // 2], 16 * m + 16)
                factor = p1_plus[:, ROWS * (h // 2):ROWS * (h // 2 + 1)].unsqueeze(2).broadcast_to([P, ROWS, COLS])
                x_half = xn[:, h // 2, (h % 2) * HALF:(h % 2 + 1) * HALF].rearrange("p (a b) -> p a b", a=ROWS)
                nc.gpsimd.tensor_tensor(t2[:, h % 2, :].rearrange("p (a b) -> p a b", a=ROWS),
                                        x_half, factor, ALU.mult).then_inc(t2_ready, 1)

            pool.wait_ge(small_loaded, SMALL)
            pool.wait_ge(p1_plus_ready, 1)

            def image(n, first, last):
                for kind, h in (("t2", 0), ("t1", 0), ("t2", 1), ("t1", 1), ("t2", 2), ("t2", 3), ("t1", 2),
                                ("t2", 4), ("t1", 3), ("t2", 5), ("t1", 4), ("t2", 6), ("t1", 5), ("t2", 7),
                                ("t1", 6), ("t1", 7)):
                    if kind == "t1":
                        t1_half(n, h)
                    elif not first:
                        t2_half(n - 1, h)

            images(pool, image)
            pool.wait_ge(t1_ready, 8 * N_IMG)
            pool.wait_ge(xh_ready, 4 * N_IMG)
            pool.wait_ge(xl_ready, 4 * N_IMG)
            nc.gpsimd.memset(pool_relu, 0.0).then_inc(pool_relu_zeroed, 1)
            pool.wait_ge(pool_relu_ready, 1)
            add_box(nc.gpsimd, lambda k: pool.wait_ge(pool_box_steps, k), pool_box_steps, pool_relu, pool_pair,
                    last_box[POOL_BOX].rearrange("p (w a b) -> p w a b", w=2, a=ROWS))
            pool.wait_ge(t2h_ready, 8 * LAST)
            pool.wait_ge(t2l_ready, 8 * LAST)
            for h in range(8):
                t2_half(LAST, h, last=True)

        @block.scalar
        def _(act):
            def copy(dst, src):
                return nc.scalar.activation(dst, src, ACT.Copy)

            def split_group(s, loads):
                act.wait_ge(xg_loaded, 16 * loads)
                copy(xg_hi[:, s, :], xg_raw[:]).then_inc(xh_ready, 1)

            def relu(m, f, before=None):
                if f:
                    act.wait_ge(box_steps, BOX_STEPS * (4 * m + (f if before is None else before)))
                act.wait_ge(xn_loaded[f], 16 * m + 16)
                nc.scalar.activation(relu_pad[:, :, :, LO:LO + COLS],
                                     xn[:, f, :].rearrange("p (w a b) -> p w a b", w=2, a=ROWS),
                                     ACT.Relu).then_inc(relu_ready, 1)

            def prepare(m, h):
                if h >= 2:
                    act.wait_ge(t13_done, 8 * m + h - 1)
                act.wait_ge(box_steps, BOX_STEPS * (4 * m + h // 2 + 1))
                copy(box_hi[:, h % 2, :], box[:, h % 2, :, :].rearrange("p a b -> p (a b)")).then_inc(boxh_ready, 1)
                act.wait_ge(t2_ready, 8 * m + h + 1)
                copy(t2_hi[:, h % 2, :], t2[:, h % 2, :]).then_inc(t2h_ready, 1)

            def y_high(idx, u):
                wait(act, y_turned, idx + 1)
                copy(yT_hi[:, ROWS * (u % 2):ROWS * (u % 2 + 1), CG * (u // 2):CG * (u // 2 + 1)],
                     ps_yT[:].rearrange("p (t i) -> p t i", t=ROWS)).then_inc(yth_ready, 1)

            def a_cross_part(m):
                act.wait_ge(a_done, m + 1)
                nc.scalar.activation(a_cross[:], ps_a[:, P:2 * P], ACT.Copy,
                                     scale=SCALE).then_inc(a_cross_ready, 1)

            act.wait_ge(w_loaded[0], 64)
            copy(of_groups(w_hi, BATCHES[0]), of_groups(w_raw, BATCHES[0])).then_inc(w_hi_ready, 1)
            act.wait_ge(w_zeroed, 2)
            act.wait_ge(w_hi_ready, 1)
            place_blocks(copy, conv_w_hi, w_hi, (0, 1, 2), BATCHES[0], w_hi_placed)
            split_group(0, 1)
            act.wait_ge(w_loaded[1], 64)
            copy(of_groups(w_hi, BATCHES[1]), of_groups(w_raw, BATCHES[1])).then_inc(w_hi_ready, 1)
            act.wait_ge(w_rest_zeroed_dve, 1)
            act.wait_ge(w_hi_ready, 2)
            place_blocks(copy, conv_w_hi, w_hi, (0, 1), BATCHES[1], w_hi_placed)
            split_group(1, 2)
            place_blocks(copy, conv_w_hi, w_hi, (2,), BATCHES[1], w_hi_placed)
            act.wait_ge(small_loaded, SMALL)
            copy(p7_hi[:], p7_raw[:]).then_inc(p7h_ready, 1)
            act.wait_ge(relu_zeroed, 1)

            def next_group(n, u):
                g = u // 2 + 2
                act.wait_ge(conv_done, 8 * n + u + 1)
                split_group(g % 2, 4 * n + g + 1)

            def image(n, first, last):
                m = n - 1
                for u in range(UNITS):
                    if u == 0 and not first:
                        act.wait_ge(conv_done, 8 * n + 1)
                        relu(m, 0)
                        prepare(m, 0)
                        prepare(m, 1)
                        relu(m, 1)
                    if u == 1:
                        next_group(n, u)
                        if not first:
                            a_cross_part(m)
                        else:
                            act.wait_ge(w_hi_placed_pool, 2)
                        y_high(8 * n, 0)
                    for i, (kind, h) in enumerate(EXTRAS[u]):
                        if kind == "T":
                            act.wait_ge(t1_ready, 8 * n + h + 1)
                            copy(t1T[:, 4 * h:4 * h + 4, 0, :],
                                 t1f[:, h % 2, :].rearrange("p (t c) -> p t c", t=4)).then_inc(tth_ready, 1)
                        if i == 0:
                            y_high(8 * n + u, u)
                        if kind == "F" and not first and h + 2 < 8:
                            prepare(m, h + 2)
                    if u in (2, 4) and not first:
                        relu(m, u // 2 + 1)
                    if u == 3 or (u in (5, 7) and not last):
                        next_group(n, u)

            images(act, image)
            act.wait_ge(box_steps, BOX_STEPS * 4 * LAST)
            relu(LAST, 0)
            act.wait_ge(xn_loaded[POOL_BOX], 16 * N_IMG)
            act.wait_ge(pool_relu_zeroed, 1)
            nc.scalar.activation(pool_relu[:, :, :, LO:LO + COLS],
                                 xn[:, POOL_BOX, :].rearrange("p (w a b) -> p w a b", w=2, a=ROWS),
                                 ACT.Relu).then_inc(pool_relu_ready, 1)
            a_cross_part(LAST)
            for i, f in enumerate(DVE_BOXES[1:]):
                relu(LAST, f, i + 1)

        @block.vector
        def _(dve):
            def low(dst, exact, high):
                return nc.vector.tensor_tensor(dst, exact, high.bitcast(F32), ALU.subtract)

            def split_group(idx, s):
                dve.wait_ge(xh_ready, idx + 1)
                low(xg_lo[:, s, :], xg_raw[:], xg_hi[:, s, :]).then_inc(xl_ready, 1)

            def box_sums(m, f, last=False):
                base = BOX_STEPS * (4 * m + (DVE_BOXES.index(f) if last else f))
                dve.wait_ge(relu_ready, 4 * m + (DVE_BOXES.index(f) if last else f) + 1)
                dst = box[:]
                if last:
                    dst = last_box[f].rearrange("p (w a b) -> p w a b", w=2, a=ROWS)
                    dve.wait_ge(t1_ready, 8 * N_IMG)
                elif f:
                    dve.wait_ge(boxh_ready, 8 * m + 2 * f)
                    dve.wait_ge(boxl_ready, 8 * m + 2 * f)
                add_box(nc.vector, lambda k: dve.wait_ge(box_steps, base + k), box_steps, relu_pad, pair_sum, dst)

            def prepare(m, h):
                dve.wait_ge(boxh_ready, 8 * m + h + 1)
                low(box_lo[:, h % 2, :], box[:, h % 2, :, :].rearrange("p a b -> p (a b)"),
                    box_hi[:, h % 2, :]).then_inc(boxl_ready, 1)
                dve.wait_ge(t2h_ready, 8 * m + h + 1)
                low(t2_lo[:, h % 2, :], t2[:, h % 2, :], t2_hi[:, h % 2, :]).then_inc(t2l_ready, 1)

            def y_low(idx, u):
                dve.wait_ge(yth_ready, idx + 1)
                at = (slice(None), slice(ROWS * (u % 2), ROWS * (u % 2 + 1)), slice(CG * (u // 2), CG * (u // 2 + 1)))
                low(yT_lo[at], ps_yT[:].rearrange("p (t i) -> p t i", t=ROWS), yT_hi[at]).then_inc(ytl_ready, 1)

            def t1_low(n, h):
                dve.wait_ge(tth_ready, 8 * n + h + 1)
                low(t1T[:, 4 * h:4 * h + 4, 1, :], t1f[:, h % 2, :].rearrange("p (t c) -> p t c", t=4),
                    t1T[:, 4 * h:4 * h + 4, 0, :]).then_inc(ttl_ready, 1)

            def turn_y(n, u):
                dve.wait_ge(conv_done, 8 * n + u + 1)
                wait(dve, yth_ready, 8 * n + u)
                wait(dve, ytl_ready, 8 * n + u)
                nc.vector.transpose(ps_yT[:], ps_conv[:, u % 2, :]).then_inc(y_turned, 1)

            def p7_bank(m, h):
                return last_p7_banks[h % 4] if isinstance(m, int) and m == LAST else ps_p7[:, h % 2, :]

            def base_half(m, h):
                dve.wait_ge(p7_done, 8 * m + h + 1)
                s = out_slot(m, h)
                stores = 4 * m + h // 2
                if isinstance(m, int) and m == LAST:
                    stores = h // 4 + (4 * LAST if s < 2 else 0)
                dve.wait_ge(stored[s], 16 * stores + 16)
                nc.vector.scalar_tensor_tensor(
                    out=out_slots[s], in0=p7_bank(m, h), scalar=FIFTH,
                    in1=xn[:, h // 2, (h % 2) * HALF:(h % 2 + 1) * HALF],
                    op0=ALU.mult, op1=ALU.add).then_inc(base_ready, 1)

            def max_half(m, h):
                s = out_slot(m, h)
                dve.wait_ge(t13_done, 8 * m + h + 1)
                dve.wait_ge(base_ready, 8 * m + h + 1)
                nc.vector.tensor_tensor(out_slots[s], ps_t13[:, h % 2, :], out_slots[s],
                                        ALU.max).then_inc(out_ready, 1)

            def join_aT(m):
                dve.wait_ge(a_cross_ready, m + 1)
                nc.vector.scalar_tensor_tensor(
                    out=aT[:], in0=ps_a[:, 0:P], scalar=SCALE, in1=a_cross[:],
                    op0=ALU.mult, op1=ALU.add).then_inc(aT_steps, 1)

            nc.vector.memset(relu_pad[:], 0.0).then_inc(relu_zeroed, 1)
            nc.vector.memset(conv_w_hi[:, 1:].bitcast(F32), 0.0).then_inc(w_rest_zeroed_dve, 1)
            for i, batch in enumerate(BATCHES):
                dve.wait_ge(w_hi_ready, i + 1)
                low(of_groups(w_lo, batch), of_groups(w_raw, batch), of_groups(w_hi, batch)).then_inc(w_lo_ready, 1)
                dve.wait_ge(w_rest_zeroed if i else w_zeroed, 2 - i)
                dve.wait_ge(w_lo_ready, i + 1)
                place_blocks(nc.vector.tensor_copy, conv_w_lo, w_lo, (0, 1, 2), batch, w_lo_placed)
                if i:
                    split_group(1, 1)
                place_blocks(nc.vector.tensor_copy, conv_w_lo, w_lo, (3,), batch, w_lo_placed)
                if i == 0:
                    split_group(0, 0)
            dve.wait_ge(small_loaded, SMALL)
            nc.vector.tensor_scalar_add(p1_plus[:], p1_sb[:], 1.0).then_inc(p1_plus_ready, 1)
            dve.wait_ge(p7h_ready, 1)
            low(p7_lo[:], p7_raw[:], p7_hi[:]).then_inc(p7l_ready, 1)

            def next_group(n, u):
                g = u // 2 + 2
                dve.wait_ge(conv_done, 8 * n + u + 1)
                split_group(4 * n + g, g % 2)

            def image(n, first, last):
                m = n - 1
                for u in range(UNITS):
                    if u != 1:
                        turn_y(n, u)
                    if u == 0 and not first:
                        box_sums(m, 0)
                        prepare(m, 0)
                        prepare(m, 1)
                    if u == 1:
                        next_group(n, u)
                    if u == 1 and not first:
                        box_sums(m, 1)
                        join_aT(m)
                        dve.wait_ge(aT_steps, AT_STEPS * m + 1)
                        nc.vector.tensor_copy(aT_hi[:], aT[:]).then_inc(aT_steps, 1)
                        dve.wait_ge(aT_steps, AT_STEPS * m + 2)
                        low(aT_lo[:], aT[:], aT_hi[:]).then_inc(aT_steps, 1)
                    if u == 1:
                        y_low(8 * n, 0)
                        turn_y(n, 1)
                    if last and u == UNITS - 1:
                        t1_low(n, 6)
                        t1_low(n, 7)
                        y_low(8 * n + u, u)
                        base_half(m, 5)
                        max_half(m, 5)
                        prepare(m, 7)
                        base_half(m, 6)
                        max_half(m, 6)
                        continue
                    if last and u == UNITS - 2:
                        base_half(m, 4)
                        max_half(m, 4)
                        y_low(8 * n + u, u)
                        prepare(m, 6)
                        t1_low(n, 5)
                        continue
                    for kind, h in EXTRAS[u]:
                        if kind == "T" and u != 6:
                            t1_low(n, h)
                        elif kind == "F" and not first:
                            base_half(m, h)
                            max_half(m, h)
                        if kind == "F" or u == 1:
                            if h == FIRST_F[u] and u != 6:
                                y_low(8 * n + u, u)
                            if not first and h + 2 < 8 and kind == "F":
                                prepare(m, h + 2)
                    if u == 6:
                        next_group(n, 5)
                        y_low(8 * n + u, u)
                        t1_low(n, 5)
                    if u in (3, 5) and not first:
                        box_sums(m, (u + 1) // 2)
                    if u == 3 or (u == 7 and not last):
                        next_group(n, u)

            images(dve, image)
            box_sums(LAST, 0, last=True)
            join_aT(LAST)
            base_half(LAST - 1, 7)
            max_half(LAST - 1, 7)
            base_half(LAST, 0)
            base_half(LAST, 1)
            box_sums(LAST, 2, last=True)
            for h in (0, 1):
                base_half(LAST, h + 2)
                max_half(LAST, h)
            box_sums(LAST, 3, last=True)
            max_half(LAST, 2)
            max_half(LAST, 3)
            for h in range(4, 8):
                base_half(LAST, h)
                max_half(LAST, h)

        @block.tensor
        def _(pe):
            def products(dst, w_parts, x_parts, start, stop):
                (wh, wl), (xh, xl) = w_parts, x_parts
                nc.tensor.matmul(dst, wh, xh, start=start, stop=False)
                nc.tensor.matmul(dst, wh, xl, start=False, stop=False)
                return nc.tensor.matmul(dst, wl, xh, start=False, stop=stop)

            def conv_unit(n, u):
                g, q = u // 2, u % 2
                pe.wait_ge(xh_ready, 4 * n + g + 1)
                pe.wait_ge(xl_ready, 4 * n + g + 1)
                wait(pe, y_turned, 8 * n + u - 1)
                xs = [part[:, g % 2, :].rearrange("p (a b) -> p a b", a=BH) for part in (xg_hi, xg_lo)]
                for jh in range(JH):
                    for jw in range(JW):
                        view = [x[:, q * ROWS + jh:q * ROWS + jh + ROWS, jw:jw + COLS] for x in xs]
                        last = products(ps_conv[:, q, :].rearrange("p (a b) -> p a b", a=ROWS),
                                        (conv_w_hi[:, g, jh, jw, :], conv_w_lo[:, g, jh, jw, :]), view,
                                        start=(jh == 0 and jw == 0), stop=(jh == JH - 1 and jw == JW - 1))
                last.then_inc(conv_done, 1)

            def y_times_t1(m):
                pe.wait_ge(yth_ready, 8 * m + 8)
                pe.wait_ge(ytl_ready, 8 * m + 8)
                pe.wait_ge(tth_ready, 8 * m + 8)
                pe.wait_ge(ttl_ready, 8 * m + 8)
                for t in range(TILES):
                    nc.tensor.matmul(ps_a[:, :], yT_hi[:, t, :], t1T[:, t, :, :].rearrange("p s c -> p (s c)"),
                                     start=(t == 0), stop=False)
                    last = nc.tensor.matmul(ps_a[:, P:2 * P], yT_lo[:, t, :], t1T[:, t, 0, :],
                                            start=False, stop=(t == TILES - 1))
                last.then_inc(a_done, 1)

            def output_half(m, h):
                s = h % 2
                pe.wait_ge(boxh_ready, 8 * m + h + 1)
                pe.wait_ge(boxl_ready, 8 * m + h + 1)
                if h >= 2:
                    pe.wait_ge(out_ready, 8 * m + h - 1)
                pe.wait_ge(aT_steps, AT_STEPS * m + AT_STEPS)
                products(ps_p7[:, s, :], (p7_hi[:], p7_lo[:]), (box_hi[:, s, :], box_lo[:, s, :]),
                         True, True).then_inc(p7_done, 1)
                pe.wait_ge(t2h_ready, 8 * m + h + 1)
                pe.wait_ge(t2l_ready, 8 * m + h + 1)
                products(ps_t13[:, s, :], (aT_hi[:], aT_lo[:]), (t2_hi[:, s, :], t2_lo[:, s, :]),
                         True, True).then_inc(t13_done, 1)

            def last_p7(h):
                f = h // 2
                if f == POOL_BOX:
                    pe.wait_ge(pool_box_steps, BOX_STEPS)
                else:
                    pe.wait_ge(box_steps, BOX_STEPS * (4 * LAST + DVE_BOXES.index(f) + 1))
                pe.wait_ge(base_ready, 8 * LAST + h - 3)
                nc.tensor.matmul(last_p7_banks[h % 4], p7_raw[:], last_box[f][:, (h % 2) * HALF:(h % 2 + 1) * HALF],
                                 start=True, stop=True).then_inc(p7_done, 1)

            def last_t13(h):
                pe.wait_ge(aT_steps, AT_STEPS * LAST + 1)
                pe.wait_ge(t2_ready, 8 * LAST + h + 1)
                pe.wait_ge(out_ready, 8 * LAST + h - 1)
                nc.tensor.matmul(ps_t13[:, h % 2, :], aT[:], t2[:, h % 2, :],
                                 start=True, stop=True).then_inc(t13_done, 1)

            def image(n, first, last):
                for u in range(UNITS):
                    if first and u in (0, 2):
                        pe.wait_ge(w_hi_placed, u + 1)
                        pe.wait_ge(w_hi_placed_pool, u // 2 + 1)
                        pe.wait_ge(w_lo_placed, u + 2)
                    conv_unit(n, u)
                    if first and u == 1:
                        pe.wait_ge(p7h_ready, 1)
                        pe.wait_ge(p7l_ready, 1)
                    if u == 1 and not first:
                        y_times_t1(n - 1)
                    for kind, h in EXTRAS[u]:
                        if kind == "F" and not first and not (last and h == 7):
                            output_half(n - 1, h)

            pe.wait_ge(relu_zeroed, 1)
            zeros = relu_pad[:].rearrange("p w a b -> p (w a b)")
            for _ in range(WARM_UP):
                nc.tensor.matmul(ps_a[:, :], zeros[:, 0:P], zeros[:, 0:2 * P], start=True, stop=True)

            images(pe, image)
            y_times_t1(LAST)
            output_half(LAST - 1, 7)
            for h in range(4):
                last_p7(h)
            last_t13(0)
            last_t13(1)
            for h in range(2, 8):
                if h + 2 < 8:
                    last_p7(h + 2)
                last_t13(h)


def add_box(engine, wait_step, steps, relu, pair, dst):
    engine.tensor_tensor(pair[:, 0], relu[:, 0, :, 0:PS_W], relu[:, 1, :, 1:1 + PS_W], ALU.add).then_inc(steps, 1)
    engine.tensor_tensor(pair[:, 1], relu[:, 1, :, 0:PS_W], relu[:, 0, :, 2:2 + PS_W], ALU.add).then_inc(steps, 1)
    wait_step(2)
    engine.tensor_tensor(dst, pair[:, :, :, 0:COLS], pair[:, :, :, LO:LO + COLS], ALU.add).then_inc(steps, 1)
    wait_step(3)
    engine.tensor_tensor(dst, dst, relu[:, :, :, 2 * LO:2 * LO + COLS], ALU.add).then_inc(steps, 1)


def place_blocks(copy, blocks, taps, uvs, groups, done):
    src = taps.rearrange("p (g t i) -> p g t i", g=GROUPS, t=TAPS)
    g0, g1 = groups
    last = None
    for b in uvs:
        u, v = b // 2, b % 2
        for r in range(4):
            rh, rw = r // 2, r % 2
            js = [j for j in range(JW) if 0 <= 2 * j + v - rw < KW]
            for jh in range(JH):
                dh = 2 * jh + u - rh
                if not 0 <= dh < KH:
                    continue
                lo = KW * dh + 2 * js[0] + v - rw
                last = copy(blocks[CG * b:CG * (b + 1), g0:g1, jh, js[0]:js[-1] + 1, CG * r:CG * (r + 1)],
                            src[CG * b:CG * (b + 1), g0:g1, lo:lo + 2 * len(js) - 1:2, :])
    last.then_inc(done, 1)


def kernel(**inputs):
    import numpy as np
    import concourse.bacc as bacc
    from concourse.bass_utils import run_bass_kernel_spmd

    x = np.asarray(inputs["x"])
    p1 = np.asarray(inputs["L0_conv_p1_w"])
    p7 = np.asarray(inputs["L0_conv_p7_w"])
    p10 = np.asarray(inputs["L0_conv_p10_w"])
    x_nat = np.ascontiguousarray(
        x.reshape(N_IMG, C, 2, ROWS, 2, COLS, 2).transpose(0, 1, 4, 2, 6, 3, 5)).reshape(N_IMG, C, FS, 2 * HALF)
    x_pix = np.ascontiguousarray(
        x.reshape(N_IMG, C, 4, 8, 2, COLS, 2).transpose(0, 2, 4, 6, 5, 3, 1)).reshape(N_IMG, FS, P, 2 * HALF)
    xp = np.pad(x, ((0, 0), (0, 0), (1, 1), (3, 3)))
    x_conv = np.ascontiguousarray(
        xp.reshape(N_IMG, GROUPS, CG, BH, 2, BW, 2).transpose(0, 1, 4, 6, 2, 3, 5)).reshape(N_IMG, GROUPS, P, XG)
    arrays = {
        "x_nat": x_nat,
        "x_pix": x_pix,
        "x_conv": x_conv,
        "p1": np.ascontiguousarray(p1.reshape(C, H // 2, 2).transpose(0, 2, 1)).reshape(C, H),
        "p1T": np.ascontiguousarray(p1.reshape(C, H // 2, 2).transpose(2, 1, 0)),
        "p7T": np.ascontiguousarray(p7.T),
        "p10": np.ascontiguousarray(p10),
    }
    nc = bacc.Bacc("TRN2", target_bir_lowering=False, num_devices=1)
    args = [nc.dram_tensor(name, a.shape, F32, kind="ExternalInput").ap() for name, a in arrays.items()]
    out = nc.dram_tensor("out", (N_IMG, C, FS, 2 * HALF), F32, kind="ExternalOutput").ap()
    conv_seq_kernel(nc, *args, out)
    result = run_bass_kernel_spmd(nc, [arrays], core_ids=[0]).results[0]["out"]
    return np.ascontiguousarray(
        result.reshape(N_IMG, C, 2, 2, 2, ROWS, COLS).transpose(0, 1, 3, 5, 2, 6, 4)).reshape(N_IMG, C, H, W)
```
